# Optimizing a Trainium2 kernel written in Bass

```python
import numpy as np
import jax
import jax.numpy as jnp

def _softmax(x, axis=-1):
    return jax.nn.softmax(x, axis=axis)

def _gelu(x):
    return jax.nn.gelu(x, approximate=True)

def _silu(x):
    return jax.nn.silu(x)

def _sigmoid(x):
    return jax.nn.sigmoid(x)

def _layernorm(x, axis=-1, eps=1e-05):
    m = jnp.mean(x, axis=axis, keepdims=True)
    v = jnp.var(x, axis=axis, keepdims=True)
    return (x - m) / jnp.sqrt(v + eps)

def _scatter_add(tgt, idx, src, axis=0):
    return tgt.at[idx].add(src)

def _segment_sum(src, seg, n):
    return jax.ops.segment_sum(src, seg, n)
kernel_name = 'mk_prb_d1_jaxref_r8_ecc877'

def setup_inputs(seed: int=0):
    np.random.seed(seed)
    _w = jnp.asarray

    def _L0_attn_setup():
        import jax, jax.numpy as jnp
        import numpy as np
        LN_EPS = 1e-05
        WKV_EPS = 1e-08
        NEG_INF = -1e+38

        def _layernorm(x, g, b):
            m = jnp.mean(x, axis=-1, keepdims=True)
            v = jnp.mean(jnp.square(x - m), axis=-1, keepdims=True)
            return (x - m) * jax.lax.rsqrt(v + LN_EPS) * g + b

        def _wkv(w, u, k, v):
            B, T, C = k.shape
            aa0 = jnp.zeros((B, C), k.dtype)
            bb0 = jnp.full((B, C), NEG_INF, k.dtype)

            def step(carry, kv_t):
                aa, bb = carry
                kk, vv = kv_t
                ww = u + kk
                p = jnp.maximum(bb, ww)
                e1 = jnp.exp(bb - p)
                e2 = jnp.exp(ww - p)
                y_t = (e1 * aa + e2 * vv) / (e1 + e2 + WKV_EPS)
                ww = w + bb
                p = jnp.maximum(ww, kk)
                e1 = jnp.exp(ww - p)
                e2 = jnp.exp(kk - p)
                aa = e1 * aa + e2 * vv
                bb = p + jnp.log(e1 + e2 + WKV_EPS)
                return ((aa, bb), y_t)
            (aa, bb), ys = jax.lax.scan(step, (aa0, bb0), (jnp.swapaxes(k, 0, 1), jnp.swapaxes(v, 0, 1)))
            y = jnp.swapaxes(ys, 0, 1)
            new_state = jnp.stack([aa, bb], axis=-1)
            return (y, new_state)

        def _reference_tuple_inner(x, time_decay, time_first, W_tm, g1, b1, tmk, tmv, tmr, W_cm, W_cp, g2, b2, cmk, cmr):
            x_prev = jnp.concatenate([x[:, :1], x[:, :-1]], axis=1)
            kvr = _layernorm(x, g1, b1) @ W_tm
            k, v, r = jnp.split(kvr, 3, axis=-1)
            k = k * tmk + x_prev * (1.0 - tmk)
            v = v * tmv + x_prev * (1.0 - tmv)
            r = jax.nn.sigmoid(r * tmr + x_prev * (1.0 - tmr))
            y, new_state = _wkv(time_decay, time_first, k, v)
            x = x + r * y
            xp = jnp.concatenate([x[:, -1:], x[:, :-1]], axis=1)
            xn = _layernorm(x, g2, b2)
            kk = xn @ W_cm
            cmk4 = jnp.tile(cmk, (1, 1, 4))
            xp4 = jnp.tile(xp, (1, 1, 4))
            kk = kk * cmk4 + xp4 * (1.0 - cmk4)
            rr = jax.nn.sigmoid(xn * cmr + xp * (1.0 - cmr))
            vv = jnp.square(jax.nn.relu(kk)) @ W_cp
            x = x + rr * vv
            return (x, new_state)
        key = jax.random.key(seed)
        ks = jax.random.split(key, 12)
        B, T, C = (8, 256, 128)
        scale = 0.02
        return {'x': jax.random.normal(ks[0], (B, T, C), jnp.float32), 'time_decay': jax.random.uniform(ks[1], (C,), jnp.float32, -1.0, 1.0), 'time_first': jax.random.uniform(ks[2], (C,), jnp.float32, -1.0, 1.0), 'W_tm': jax.random.normal(ks[3], (C, 3 * C), jnp.float32) * scale, 'g1': jnp.ones((C,), jnp.float32), 'b1': jnp.zeros((C,), jnp.float32), 'tmk': jax.random.uniform(ks[4], (1, 1, C), jnp.float32), 'tmv': jax.random.uniform(ks[5], (1, 1, C), jnp.float32), 'tmr': jax.random.uniform(ks[6], (1, 1, C), jnp.float32), 'W_cm': jax.random.normal(ks[7], (C, 4 * C), jnp.float32) * scale, 'W_cp': jax.random.normal(ks[8], (4 * C, C), jnp.float32) * scale, 'g2': jnp.ones((C,), jnp.float32), 'b2': jnp.zeros((C,), jnp.float32), 'cmk': jax.random.uniform(ks[9], (1, 1, C), jnp.float32), 'cmr': jax.random.uniform(ks[10], (1, 1, C), jnp.float32)}
    _L0_attn_in = _L0_attn_setup()

    def _L0_ffn_setup():
        import jax, jax.numpy as jnp
        import numpy as np
        B, S, H = (4, 256, 128)
        E = 8
        GS = 2
        NG = E // GS
        F = int(H * 4 * (2.0 / 3.0))
        key = jax.random.key(seed)
        ks = jax.random.split(key, 7)
        sc_h = 1.0 / np.sqrt(H)
        sc_f = 1.0 / np.sqrt(F)
        return {'x': jax.random.normal(ks[0], (B, S, H), dtype=jnp.float32), 'Wr': jax.random.normal(ks[1], (H, E), dtype=jnp.float32) * sc_h, 'br': jnp.zeros((E,), dtype=jnp.float32), 'W_up': jax.random.normal(ks[2], (NG, H, F), dtype=jnp.float32) * sc_h, 'b_up': jax.random.normal(ks[3], (NG, F), dtype=jnp.float32) * 0.01, 'W_down': jax.random.normal(ks[4], (E, F, H), dtype=jnp.float32) * sc_f, 'b_down': jax.random.normal(ks[5], (E, H), dtype=jnp.float32) * 0.01}
    _L0_ffn_in = _L0_ffn_setup()
    _d = {'L0_attn_x': _L0_attn_in['x'], 'L0_attn_time_decay': _L0_attn_in['time_decay'], 'L0_attn_time_first': _L0_attn_in['time_first'], 'L0_attn_W_tm': _L0_attn_in['W_tm'], 'L0_attn_g1': _L0_attn_in['g1'], 'L0_attn_b1': _L0_attn_in['b1'], 'L0_attn_tmk': _L0_attn_in['tmk'], 'L0_attn_tmv': _L0_attn_in['tmv'], 'L0_attn_tmr': _L0_attn_in['tmr'], 'L0_attn_W_cm': _L0_attn_in['W_cm'], 'L0_attn_W_cp': _L0_attn_in['W_cp'], 'L0_attn_g2': _L0_attn_in['g2'], 'L0_attn_b2': _L0_attn_in['b2'], 'L0_attn_cmk': _L0_attn_in['cmk'], 'L0_attn_cmr': _L0_attn_in['cmr'], 'L0_ffn_Wr': _L0_ffn_in['Wr'], 'L0_ffn_br': _L0_ffn_in['br'], 'L0_ffn_W_up': _L0_ffn_in['W_up'], 'L0_ffn_b_up': _L0_ffn_in['b_up'], 'L0_ffn_W_down': _L0_ffn_in['W_down'], 'L0_ffn_b_down': _L0_ffn_in['b_down']}
    _x0 = _d['L0_attn_x']
    _d['L0_attn_x'] = jax.random.normal(jax.random.fold_in(jax.random.key(seed), 1), (8, 512, 128), dtype=_x0.dtype)
    del _x0
    return _d

def reference(L0_attn_x, L0_attn_time_decay, L0_attn_time_first, L0_attn_W_tm, L0_attn_g1, L0_attn_b1, L0_attn_tmk, L0_attn_tmv, L0_attn_tmr, L0_attn_W_cm, L0_attn_W_cp, L0_attn_g2, L0_attn_b2, L0_attn_cmk, L0_attn_cmr, L0_ffn_Wr, L0_ffn_br, L0_ffn_W_up, L0_ffn_b_up, L0_ffn_W_down, L0_ffn_b_down):

    def _L0_attn_ref(x, time_decay, time_first, W_tm, g1, b1, tmk, tmv, tmr, W_cm, W_cp, g2, b2, cmk, cmr):
        import jax, jax.numpy as jnp
        import numpy as np
        LN_EPS = 1e-05
        WKV_EPS = 1e-08
        NEG_INF = -1e+38

        def _layernorm(x, g, b):
            m = jnp.mean(x, axis=-1, keepdims=True)
            v = jnp.mean(jnp.square(x - m), axis=-1, keepdims=True)
            return (x - m) * jax.lax.rsqrt(v + LN_EPS) * g + b

        def _wkv(w, u, k, v):
            B, T, C = k.shape
            aa0 = jnp.zeros((B, C), k.dtype)
            bb0 = jnp.full((B, C), NEG_INF, k.dtype)

            def step(carry, kv_t):
                aa, bb = carry
                kk, vv = kv_t
                ww = u + kk
                p = jnp.maximum(bb, ww)
                e1 = jnp.exp(bb - p)
                e2 = jnp.exp(ww - p)
                y_t = (e1 * aa + e2 * vv) / (e1 + e2 + WKV_EPS)
                ww = w + bb
                p = jnp.maximum(ww, kk)
                e1 = jnp.exp(ww - p)
                e2 = jnp.exp(kk - p)
                aa = e1 * aa + e2 * vv
                bb = p + jnp.log(e1 + e2 + WKV_EPS)
                return ((aa, bb), y_t)
            (aa, bb), ys = jax.lax.scan(step, (aa0, bb0), (jnp.swapaxes(k, 0, 1), jnp.swapaxes(v, 0, 1)))
            y = jnp.swapaxes(ys, 0, 1)
            new_state = jnp.stack([aa, bb], axis=-1)
            return (y, new_state)

        def _reference_tuple_inner(x, time_decay, time_first, W_tm, g1, b1, tmk, tmv, tmr, W_cm, W_cp, g2, b2, cmk, cmr):
            x_prev = jnp.concatenate([x[:, :1], x[:, :-1]], axis=1)
            kvr = _layernorm(x, g1, b1) @ W_tm
            k, v, r = jnp.split(kvr, 3, axis=-1)
            k = k * tmk + x_prev * (1.0 - tmk)
            v = v * tmv + x_prev * (1.0 - tmv)
            r = jax.nn.sigmoid(r * tmr + x_prev * (1.0 - tmr))
            y, new_state = _wkv(time_decay, time_first, k, v)
            x = x + r * y
            xp = jnp.concatenate([x[:, -1:], x[:, :-1]], axis=1)
            xn = _layernorm(x, g2, b2)
            kk = xn @ W_cm
            cmk4 = jnp.tile(cmk, (1, 1, 4))
            xp4 = jnp.tile(xp, (1, 1, 4))
            kk = kk * cmk4 + xp4 * (1.0 - cmk4)
            rr = jax.nn.sigmoid(xn * cmr + xp * (1.0 - cmr))
            vv = jnp.square(jax.nn.relu(kk)) @ W_cp
            x = x + rr * vv
            return (x, new_state)
        return _reference_tuple_inner(x, time_decay, time_first, W_tm, g1, b1, tmk, tmv, tmr, W_cm, W_cp, g2, b2, cmk, cmr)[0]

    def _L0_ffn_ref(x, Wr, br, W_up, b_up, W_down, b_down):
        import jax, jax.numpy as jnp
        import numpy as np
        B, S, H = (4, 256, 128)
        E = 8
        GS = 2
        NG = E // GS
        F = int(H * 4 * (2.0 / 3.0))
        b, s, h = x.shape
        n_tok = b * s
        k = n_tok // E
        xf = x.reshape(n_tok, h)
        logits = xf @ Wr + br
        Sm = jax.nn.softmax(logits, axis=-1)
        G_t, idx_t = jax.lax.top_k(Sm.T, k)
        G = G_t.T
        idx = idx_t.T
        tokens = xf[idx]
        group = jnp.arange(E) // GS
        Wu = W_up[group]
        bu = b_up[group]
        mid = jax.nn.silu(jnp.einsum('keh,ehf->kef', tokens, Wu) + bu)
        out = jnp.einsum('kef,efh->keh', mid, W_down) + b_down
        y = jnp.zeros_like(xf).at[idx].add(G[..., None] * out)
        return y.reshape(b, s, h)
    x = L0_attn_x
    xn = _layernorm(x, axis=-1)
    x = x + _L0_attn_ref(xn, L0_attn_time_decay, L0_attn_time_first, L0_attn_W_tm, L0_attn_g1, L0_attn_b1, L0_attn_tmk, L0_attn_tmv, L0_attn_tmr, L0_attn_W_cm, L0_attn_W_cp, L0_attn_g2, L0_attn_b2, L0_attn_cmk, L0_attn_cmr) + _L0_ffn_ref(xn, L0_ffn_Wr, L0_ffn_br, L0_ffn_W_up, L0_ffn_b_up, L0_ffn_W_down, L0_ffn_b_down)
    return x

_drawn_inputs = setup_inputs


def setup_inputs(seed=0):
    import zlib

    import numpy as np

    out = dict(_drawn_inputs(seed))
    spreads = {'L0_attn_g1': (1.0, 0.2),
     'L0_attn_b1': (0.0, 0.1),
     'L0_attn_g2': (1.0, 0.6),
     'L0_attn_b2': (0.0, 0.387),
     'L0_ffn_br': (0.0, 0.8)}
    factors = {'L0_attn_W_cm': 3.711, 'L0_ffn_b_up': 64.0, 'L0_ffn_b_down': 64.0}
    for name, (base, spread) in spreads.items():
        noise = np.random.default_rng([zlib.crc32(name.encode()), seed]).standard_normal(out[name].shape)
        drawn = base * np.exp(spread * noise) if base else spread * noise
        out[name] = jnp.asarray(drawn.astype(out[name].dtype))
    for name, factor in factors.items():
        out[name] = (out[name] * factor).astype(out[name].dtype)
    return out
```

```python
from contextlib import ExitStack

import concourse.bass as bass
from concourse import mybir

ALU = mybir.AluOpType
ACT = mybir.ActivationFunctionType
F32 = mybir.dt.float32
F16 = mybir.dt.float16
BF16 = mybir.dt.bfloat16
I32 = mybir.dt.int32
U32 = mybir.dt.uint32
AX = mybir.AxisListType

PARAMS = ["time_decay", "time_first", "g1", "b1", "tmk", "tmv", "tmr", "g2", "b2", "cmk", "cmr"]


def rwkv_plus_expert_choice(nc, x, time_decay, time_first, W_tm, g1, b1, tmk, tmv, tmr, W_cm, W_cp,
                            g2, b2, cmk, cmr, Wr, br, W_up, b_up, W_down, b_down, out):
    B, T, C = x.shape
    E = Wr.shape[1]
    NGRP, _, F = W_up.shape
    EG = E // NGRP
    P = 128
    assert C == P and T == 4 * P and E == B and EG == 2
    Q = T // P
    NTOK = B * T
    NF = B * Q
    KTOP = NTOK // E
    NG = KTOP // P
    FJ = [min(P, F - P * j) for j in range((F + P - 1) // P)]
    NJ = W_cm.shape[1] // C
    TP = T + 2
    ROW = C + E
    PAIRS = B // 2
    LN_EPS, WKV_EPS, NEG_INF = 1e-5, 1e-8, -1e38
    LO, HI = 32, KTOP // 32

    TINY = 2.0 ** -126
    exp_factors = [2.0 ** k for k in (64, 32, 16, 8, 4, 2, 1)] + [1.0, 1.0]
    EXP_STEPS = 8
    MAN_STEPS = 24

    xn_rows = nc.dram_tensor("xn_rows", [NTOK, ROW], F32, kind="Internal").ap()
    y_base = nc.dram_tensor("y_base", [NTOK, C], F32, kind="Internal").ap()
    x_v = x.rearrange("b (p q) c -> b p (q c)", q=Q)
    out_v = out.rearrange("b (p q) c -> b p (q c)", q=Q)
    base_v = y_base.rearrange("(b p q) c -> b p (q c)", p=P, q=Q)
    rows_v = xn_rows.rearrange("(b p q) c -> b p q c", p=P, q=Q)

    ctx = ExitStack()
    with ctx:
        def sb(name, shape, dt=F32):
            return ctx.enter_context(nc.sbuf_tensor(name, shape, dt))

        def pb(name, shape, dt=F32):
            return ctx.enter_context(nc.psum_tensor(name, shape, dt))

        def sem(name):
            return ctx.enter_context(nc.semaphore(name))

        xtok = sb("xtok", [P, B, T])
        htok = sb("htok", [P, B, T])
        xT = sb("xT", [P, B, TP])
        kd = sb("kd", [P, B, T])
        st = sb("st", [P, B, TP])
        vb = sb("vb", [P, B, T])
        rb = sb("rb", [P, B, T])
        ca = sb("ca", [P, B, T])
        cb = sb("cb", [P, B, T])
        hT = sb("hT", [P, 2, T])
        rel = sb("rel", [P, NJ, T])
        yb = sb("yb", [P, 2, T])

        par = sb("par", [P, len(PARAMS)])
        om = sb("om", [P, len(PARAMS)])
        col = {n: par[:, i:i + 1] for i, n in enumerate(PARAMS)}
        omc = {n: om[:, i:i + 1] for i, n in enumerate(PARAMS)}
        wrow = sb("wrow", [P, T])
        mixrow = sb("mixrow", [P, 3 * C])
        cmkrow = sb("cmkrow", [P, C])
        wtm = sb("wtm", [P, 3 * C])
        wcm = sb("wcm", [P, NJ * C])
        wcp = sb("wcp", [P, NJ, C])
        wr = sb("wr", [P, E])
        brr = sb("brr", [1, E])
        wup = sb("wup", [P, NGRP, F])
        bup = sb("bup", [P, NGRP, len(FJ)])
        bcur = sb("bcur", [P, len(FJ)])
        wdn = sb("wdn", [P, E, len(FJ), C])
        ident = sb("ident", [P, P])
        ones = sb("ones", [P, P], BF16)
        upper = sb("upper", [P, P], BF16)
        onerow = sb("onerow", [1, P])
        nhalf = sb("nhalf", [P, 2 * Q])
        weps = sb("weps", [P, 1])

        stats = sb("stats", [P, NF, 6])
        mv = sb("mv", [P, NF, 2])
        rs1 = sb("rs1", [P, NF])
        rs2 = sb("rs2", [P, NF])
        pw = sb("pw", [P, 2 * Q])
        pw2 = sb("pw2", [P, 2 * Q])

        prob = sb("prob", [P, NF, E])
        pcl = sb("pcl", [P, NF, E])
        rmax = sb("rmax", [P, NF])
        thr = sb("thr", [P, E])
        cand = sb("cand", [P, E])
        step = sb("step", [P, E])
        cnt = sb("cnt", [P, E])
        factor = sb("factor", [P, len(exp_factors) + MAN_STEPS])
        cmp = sb("cmp", [P, E, NF], BF16)
        gt = sb("gt", [P, E, NF])
        eq = sb("eq", [P, E, NF])
        sc = sb("sc", [P, E * NF])
        sd = sb("sd", [P, E * NF])
        restart_q = sb("restart_q", [P, E * NF])
        restart_e = sb("restart_e", [P, E * NF])
        restart_b = sb("restart_b", [P, E * B])
        rows4 = sb("rows4", [P, E * B], BF16)
        gtc = sb("gtc", [P, E], BF16)
        selc = sb("selc", [P, E], BF16)
        bex = sb("bex", [P, E * B])
        need = sb("need", [P, E])
        slot = sb("slot", [P, E * NF], I32)
        slot_hi = sb("slot_hi", [P, E * NF], I32)
        slot_lo = sb("slot_lo", [P, E * NF], I32)
        hi16 = sb("hi16", [P, E * NF], F16)
        lo16 = sb("lo16", [P, E * NF], F16)
        tok_lo = sb("tok_lo", [P, E * NF], F16)
        tok_hi = sb("tok_hi", [P, E * NF], F16)
        oh_lo = xtok[:, :, :].rearrange("p b t -> p (b t)").bitcast(F16).rearrange("p (l n) -> p l n", l=LO)
        oh_hi = htok[:, :, :].rearrange("p b t -> p (b t)").bitcast(F16).rearrange("p (k h n) -> p k h n", k=2, h=HI)
        idxf = sb("idxf", [LO, E * HI])
        idx = sb("idx", [P, E * NG], U32)

        xt_flat = xtok[:, :, :].rearrange("p b t -> p (b t)")
        ht_flat = htok[:, :, :].rearrange("p b t -> p (b t)")
        n_g, n_x, n_y = 2 * NG * ROW, 2 * KTOP, 2 * NG * C
        gath = xt_flat[:, 0:n_g].rearrange("p (s k c) -> p s k c", s=2, k=NG)
        xg = xt_flat[:, n_g:n_g + n_x].rearrange("p (s n) -> p s n", s=2)
        yo = xt_flat[:, n_g + n_x:n_g + n_x + n_y].rearrange("p (s k c) -> p s k c", s=2, k=NG)
        mid = ht_flat[:, 0:2 * len(FJ) * KTOP].rearrange("p (s j n) -> p s j n", s=2, j=len(FJ))

        tp = [pb("tp0", [P, T]), pb("tp1", [P, T])]
        mm = [pb("mm0", [P, T]), pb("mm1", [P, T])]
        mv_ps = pb("mv_ps", [P, T])
        moe = [pb("moe0", [P, T]), pb("moe1", [P, T])]
        small = pb("small", [P, T])
        lg = small[:, 0:NF * E].rearrange("p (f e) -> p f e", e=E)
        cps = small[:, NF * E:2 * NF * E].rearrange("p (e f) -> p e f", e=E)
        tie_ps = mm[1]
        idx_ps = mm[0][0:LO, 0:E * 2 * HI].rearrange("l (e k h) -> l e k h", e=E, k=2)

        x_loaded = [sem("x_loaded0"), sem("x_loaded1")]
        w_loaded = sem("w_loaded")
        base_copied = sem("base_copied")
        pool_step = sem("pool_step")
        consts_ready = sem("consts_ready")
        dve_step = sem("dve_step")
        act_step = sem("act_step")
        bias_ready = sem("bias_ready")
        weights_ready = sem("weights_ready")
        var_ready = sem("var_ready")
        rstd_ready = sem("rstd_ready")
        xn_ready = sem("xn_ready")
        h_ready = sem("h_ready")
        rows_stored = sem("rows_stored")
        xT_psum = sem("xT_psum")
        hT_psum = sem("hT_psum")
        xT_ready = sem("xT_ready")
        hT_ready = sem("hT_ready")
        logits_psum = sem("logits_psum")
        k_psum = sem("k_psum")
        v_psum = sem("v_psum")
        r_psum = sem("r_psum")
        k_ready = sem("k_ready")
        v_ready = sem("v_ready")
        r_ready = sem("r_ready")
        m_ready = sem("m_ready")
        ab_ready = sem("ab_ready")
        abexp_ready = sem("abexp_ready")
        s_ready = sem("s_ready")
        lns_ready = sem("lns_ready")
        e_ready = sem("e_ready")
        eexp_ready = sem("eexp_ready")
        aa_ready = sem("aa_ready")
        gates_ready = sem("gates_ready")
        x1_ready = sem("x1_ready")
        lmax_ready = sem("lmax_ready")
        lexp_ready = sem("lexp_ready")
        prob_ready = sem("prob_ready")
        cmp_ready = sem("cmp_ready")
        count_psum = sem("count_psum")
        ties_ready = sem("ties_ready")
        ties_psum = sem("ties_psum")
        selc_ready = sem("selc_ready")
        selc_psum = sem("selc_psum")
        onehot_ready = sem("onehot_ready")
        idx_psum = sem("idx_psum")
        idx_ready = sem("idx_ready")
        gathered = [sem("gathered0"), sem("gathered1")]
        gT_psum = sem("gT_psum")
        xg_ready = sem("xg_ready")
        up_psum = sem("up_psum")
        mid_ready = sem("mid_ready")
        down_psum = sem("down_psum")
        yo_ready = sem("yo_ready")
        scattered = [sem("scattered0"), sem("scattered1")]
        yo_added = sem("yo_added")
        x1tok_psum = sem("x1tok_psum")
        x1tok_ready = sem("x1tok_ready")
        var2_ready = sem("var2_ready")
        rstd2_ready = sem("rstd2_ready")
        xn2_ready = sem("xn2_ready")
        xn2T_psum = sem("xn2T_psum")
        xn2T_ready = sem("xn2T_ready")
        z_ready = sem("z_ready")
        rr_ready = sem("rr_ready")
        kk_psum = sem("kk_psum")
        kk_ready = sem("kk_ready")
        sq_ready = sem("sq_ready")
        vv_psum = sem("vv_psum")
        x2_ready = sem("x2_ready")
        x2tok_psum = sem("x2tok_psum")
        base_loaded = [sem("base_loaded0"), sem("base_loaded1")]
        res_ready = sem("res_ready")
        out_stored = [sem("out_stored0"), sem("out_stored1")]

        loads = [(par[:, i:i + 1], a.rearrange("(c o) -> c o", o=1)) for i, a in enumerate(
            [time_decay, time_first, g1, b1, tmk, tmv, tmr, g2, b2, cmk, cmr])]
        loads += [(mixrow[:, C * i:C * i + C], a.rearrange("(o c) -> o c", o=1).broadcast_to([P, C]))
                  for i, a in enumerate([tmk, tmv, tmr])]
        loads += [(cmkrow[:, :], cmk.rearrange("(o c) -> o c", o=1).broadcast_to([P, C])),
                  (wtm[:, :], W_tm), (wr[:, :], Wr), (brr[:, :], br.rearrange("(o e) -> o e", o=1)),
                  (wcm[:, :], W_cm), (wcp[:, :, :], W_cp.rearrange("(j k) c -> k j c", j=NJ)),
                  (wup[:, :, :], W_up.rearrange("g h f -> h g f"))]
        for j, fj in enumerate(FJ):
            loads.append((bup[0:fj, :, j:j + 1], b_up[:, P * j:P * j + fj].rearrange("g (f o) -> f g o", o=1)))
            loads.append((wdn[0:fj, :, j, :], W_down[:, P * j:P * j + fj, :].rearrange("e f c -> f e c")))
        loads.append((wdn[FJ[-1]:FJ[-1] + 1, :, len(FJ) - 1, :], b_down.rearrange("(o e) c -> o e c", o=1)))
        N_LOADS = 16 * len(loads)

        block = ctx.enter_context(nc.Block())

        @block.sync
        def _(sp):
            for s in range(2):
                sp.dma_start(xtok[:, s, :], x_v[s, :, :]).then_inc(x_loaded[s], 16)
            with sp.Fori(1, PAIRS) as i:
                for s in range(2):
                    sp.wait_ge(x_loaded[s], i * 16)
                    sp.dma_start(xtok[:, i * 2 + s, :], x_v[i * 2 + s, :, :]).then_inc(x_loaded[s], 16)
            sp.dma_start(y_base.rearrange("(a n) c -> a (n c)", a=16),
                         x.rearrange("b (h t) c -> (b h) (t c)", h=2)).then_inc(base_copied, 16)
            with sp.Fori(0, PAIRS) as i:
                sp.wait_ge(xn_ready, i + 1)
                for s in range(2):
                    sp.dma_start(rows_v[i * 2 + s, :, :, 0:C],
                                 xtok[:, i * 2 + s, :].rearrange("p (q c) -> p q c", q=Q)).then_inc(rows_stored, 16)
            sp.wait_ge(prob_ready, 1)
            for b in range(B):
                sp.dma_start(rows_v[b, :, :, C:ROW], prob[:, Q * b:Q * b + Q, :]).then_inc(rows_stored, 16)
            sp.wait_ge(yo_added, E + 2)
            for s in range(2):
                sp.dma_start(yb[:, s, :], base_v[s, :, :]).then_inc(base_loaded[s], 16)
            with sp.Fori(0, PAIRS - 1) as i:
                for s in range(2):
                    sp.wait_ge(res_ready, i * 2 + (s + 1))
                    sp.dma_start(out_v[i * 2 + s, :, :], yb[:, s, :]).then_inc(out_stored[s], 16)
                    sp.wait_ge(out_stored[s], i * 16 + 16)
                    sp.dma_start(yb[:, s, :], base_v[i * 2 + (s + 2), :, :]).then_inc(base_loaded[s], 16)
            for s in range(2):
                sp.wait_ge(res_ready, B - 1 + s)
                sp.dma_start(out_v[B - 2 + s, :, :], yb[:, s, :]).then_inc(out_stored[s], 16)
            for s in range(2):
                sp.wait_ge(out_stored[s], 16 * PAIRS)
            sp.wait_ge(rows_stored, 16 * 2 * B)

        @block.gpsimd
        def _(pool):
            n = [0]

            def link(ins):
                n[0] += 1
                ins.then_inc(pool_step, 1)
                pool.wait_ge(pool_step, n[0])

            g = nc.gpsimd
            g.memset(st[:, :, 0:1], NEG_INF)
            g.memset(nhalf[:, :], -0.5)
            g.memset(weps[:, :], WKV_EPS)
            g.memset(onerow[:, :], 1.0)
            g.memset(ones[:, :], 1.0)
            for j, v in enumerate(exp_factors + [2.0 ** -(j + 1) for j in range(MAN_STEPS)]):
                g.memset(factor[:, j:j + 1], v)
            g.memset(restart_q[:, :], 1.0)
            g.memset(restart_e[:, :], 1.0)
            g.memset(restart_b[:, :], 1.0)
            g.memset(upper[:, :], 1.0)
            link(g.memset(ident[:, :], 0.0))
            g.memset(restart_q[:, :].rearrange("p (n q) -> p n q", q=Q)[:, :, 0:1], 0.0)
            g.memset(restart_e[:, :].rearrange("p (e f) -> p e f", e=E)[:, :, 0:1], 0.0)
            g.memset(restart_b[:, :].rearrange("p (e b) -> p e b", e=E)[:, :, 0:1], 0.0)
            g.iota(tok_lo[:, :].rearrange("p (e b q) -> p e b q", e=E, b=B), pattern=[[0, E], [0, B], [1, Q]],
                   base=0, channel_multiplier=Q, allow_small_or_imprecise_dtypes=True)
            g.iota(tok_hi[:, :].rearrange("p (e b q) -> p e b q", e=E, b=B), pattern=[[0, E], [T, B], [0, Q]],
                   base=0, channel_multiplier=0, allow_small_or_imprecise_dtypes=True)
            g.affine_select(out=upper[:, :], in_=upper[:, :], compare_op=ALU.is_gt, fill=0.0, base=0,
                            pattern=[[1, P]], channel_multiplier=-1)
            g.affine_select(out=ident[:, :], in_=ident[:, :], compare_op=ALU.not_equal, fill=1.0, base=0,
                            pattern=[[-1, P]], channel_multiplier=1).then_inc(consts_ready, 1)

            for i in range(PAIRS):
                if i:
                    pool.wait_ge(rstd_ready, i)
                pool.wait_ge(var_ready, i + 1)
                v = mv[:, bass.ts(i, 2 * Q), 1]
                r1, r2 = rs1[:, bass.ts(i, 2 * Q)], rs2[:, bass.ts(i, 2 * Q)]
                link(g.tensor_scalar(pw[:, :], v, LN_EPS, None, ALU.add))
                link(g.tensor_tensor(r1, pw[:, :], nhalf[:, :], ALU.pow))
                link(g.tensor_tensor(pw2[:, :], r1, r1, ALU.mult))
                link(g.tensor_tensor(pw2[:, :], pw2[:, :], v, ALU.mult))
                link(g.tensor_scalar(pw2[:, :], pw2[:, :], LN_EPS, None, ALU.add))
                g.tensor_tensor(r2, pw2[:, :], nhalf[:, :], ALU.pow).then_inc(rstd_ready, 1)

            for i in range(PAIRS):
                pool.wait_ge(xn_ready, i + 1)
                pool.wait_ge(rstd_ready, i + 1)
                for s in range(2):
                    for q in range(Q):
                        part = slice(P * q, P * q + P)
                        f = i * 2 * Q + Q * s + q
                        last = g.tensor_scalar(htok[:, i * 2 + s, part], xtok[:, i * 2 + s, part],
                                               rs2[:, f:f + 1], None, ALU.mult)
                last.then_inc(h_ready, 1)

            pool.wait_ge(rows_stored, 16 * 2 * B)
            pool.wait_ge(base_copied, 16)
            pool.wait_ge(idx_ready, 1)
            link(g.memset(mid[:, :, len(FJ) - 1, :], 1.0))
            pool.sem_inc(yo_added, 2)

            def gather(e):
                s = e % 2
                pool.wait_ge(yo_ready, e + 1)
                for k in range(NG):
                    g.indirect_dma_start(out=gath[:, s, k, :], out_offset=None, in_=xn_rows[:, :],
                                         in_offset=bass.IndirectOffsetOnAxis(ap=idx[:, e * NG + k:e * NG + k + 1], axis=0),
                                         ).then_inc(gathered[s], 16)

            def scatter(e):
                s = e % 2
                pool.wait_ge(yo_ready, e + 3)
                for k in range(NG):
                    g.indirect_dma_start(out=y_base[:, :],
                                         out_offset=bass.IndirectOffsetOnAxis(ap=idx[:, e * NG + k:e * NG + k + 1], axis=0),
                                         in_=yo[:, s, k, :], in_offset=None, compute_op=ALU.add).then_inc(scattered[s], 16)
                    pool.wait_ge(scattered[s], 16 * (NG * (e // 2) + k + 1))
                pool.sem_inc(yo_added, 1)

            def rstd_x1(i):
                if i:
                    pool.wait_ge(rstd2_ready, i)
                pool.wait_ge(var2_ready, i + 1)
                link(g.tensor_scalar(pw[:, :], mv[:, bass.ts(i, 2 * Q), 1], LN_EPS, None, ALU.add))
                g.tensor_tensor(rs2[:, bass.ts(i, 2 * Q)], pw[:, :], nhalf[:, :], ALU.pow).then_inc(rstd2_ready, 1)

            for e in range(2):
                gather(e)
            for e in range(E):
                scatter(e)
                if e + 2 < E:
                    gather(e + 2)
                if e % 2:
                    rstd_x1(e // 2)

        @block.scalar
        def _(act):
            a = nc.scalar
            with nc.allow_non_contiguous_dma(reason="a few hundred bias values"):
                for dst, src in loads:
                    act.dma_start(dst, src).then_inc(w_loaded, 16)
            a.preload_act_table_set("natural_log_exp_and_others")
            act.sem_inc(yo_ready, 2)
            act.wait_ge(w_loaded, N_LOADS)
            with act.Fori(0, PAIRS) as i:
                for s in range(2):
                    act.wait_ge(xT_psum, i * 2 + (s + 1))
                    a.copy(xT[:, i * 2 + s, 0:1], tp[0][:, 0:1])
                    a.copy(xT[:, i * 2 + s, 1:T + 1], tp[0][:, :]).then_inc(xT_ready, 1)
                    act.wait_ge(hT_psum, i * 2 + (s + 1))
                    act.wait_ge(r_psum, i * 2 + (s + 1))
                    a.activation(hT[:, s, :], tp[1][:, :], ACT.Identity, bias=col["b1"], scale=col["g1"]).then_inc(hT_ready, 1)
            with act.Fori(0, PAIRS) as i:
                act.wait_ge(ab_ready, i + 1)
                a.activation(ca[:, bass.ts(i, 2), :], ca[:, bass.ts(i, 2), :], ACT.Exp, scale=-1.0)
                a.activation(cb[:, bass.ts(i, 2), :], cb[:, bass.ts(i, 2), :], ACT.Exp).then_inc(abexp_ready, 1)
            act.wait_ge(lmax_ready, 1)
            a.activation(prob[:, :, :], prob[:, :, :], ACT.Exp).then_inc(lexp_ready, 1)
            with act.Fori(0, PAIRS) as i:
                act.wait_ge(s_ready, i * 2 + 2)
                a.activation(st[:, bass.ts(i, 2), 0:T], st[:, bass.ts(i, 2), 0:T], ACT.Ln,
                             bias=weps[:, 0:1]).then_inc(lns_ready, 1)
            with act.Fori(0, PAIRS) as i:
                act.wait_ge(e_ready, i + 1)
                a.activation(ca[:, bass.ts(i, 2), :], ca[:, bass.ts(i, 2), :], ACT.Exp, scale=-1.0)
                a.activation(cb[:, bass.ts(i, 2), :], cb[:, bass.ts(i, 2), :], ACT.Exp).then_inc(eexp_ready, 1)
            with act.Fori(0, PAIRS) as i:
                act.wait_ge(e_ready, i + 1)
                a.activation(kd[:, bass.ts(i, 2), :], kd[:, bass.ts(i, 2), :], ACT.Sigmoid, bias=col["time_first"])
                a.activation(rb[:, bass.ts(i, 2), :], rb[:, bass.ts(i, 2), :], ACT.Sigmoid).then_inc(gates_ready, 1)
            full = len(FJ) - 1
            with act.Fori(0, PAIRS) as i:
                a.copy(bcur[:, 0:full], bup[:, i, 0:full])
                a.copy(bcur[0:FJ[full], full:full + 1], bup[0:FJ[full], i, full:full + 1]).then_inc(bias_ready, 1)
                act.wait_ge(bias_ready, i + 1)
                for s in range(2):
                    e = i * 2 + s
                    act.wait_ge(x1tok_psum, e + 1)
                    a.copy(vb[:, e, :], tp[s][:, :]).then_inc(x1tok_ready, 1)
                    act.wait_ge(gT_psum, e + 1)
                    a.copy(xg[:, s, :], moe[s][:, :]).then_inc(xg_ready, 1)
                    for j, fj in enumerate(FJ):
                        act.wait_ge(up_psum, e * len(FJ) + (j + 1))
                        a.activation(mid[0:fj, s, j, :], moe[(s + 1 + j) % 2][0:fj, :], ACT.Silu,
                                     bias=bcur[0:fj, j:j + 1]).then_inc(mid_ready, 1)
                    act.wait_ge(down_psum, e + 1)
                    act.wait_ge(yo_added, e + 1)
                    for k in range(NG):
                        last = a.activation(yo[:, s, k, :], moe[s][:, C * k:C * k + C], ACT.Copy,
                                            scale=gath[:, s, k, bass.ds(e + C, 1)])
                    last.then_inc(yo_ready, 1)
            with act.Fori(0, PAIRS) as i:
                for s in range(2):
                    act.wait_ge(xn2T_psum, i * 2 + (s + 1))
                    a.activation(rb[:, i * 2 + s, :], tp[s][:, :], ACT.Identity, bias=col["b2"],
                                 scale=col["g2"]).then_inc(xn2T_ready, 1)
            with act.Fori(0, PAIRS) as i:
                act.wait_ge(z_ready, i + 1)
                a.activation(cb[:, bass.ts(i, 2), :], cb[:, bass.ts(i, 2), :], ACT.Sigmoid).then_inc(rr_ready, 1)
            with act.Fori(0, B) as b:
                for j in range(NJ):
                    act.wait_ge(kk_ready, b * NJ + (j + 1))
                    a.activation(rel[:, j, :], rel[:, j, :], ACT.Relu).then_inc(act_step, 1)
                    act.wait_ge(act_step, b * NJ + (j + 1))
                    a.activation(rel[:, j, :], rel[:, j, :], ACT.Square).then_inc(sq_ready, 1)

        @block.vector
        def _(dve):
            v = nc.vector
            steps = [0]
            per = [0, 0]

            def link(ins):
                per[0] += 1
                ins.then_inc(dve_step, 1)
                dve.wait_ge(dve_step, per[1] + (steps[0] + per[0]))

            def turn(i, size):
                steps[0] += per[0] if not isinstance(per[1], int) or per[1] == 0 else 0
                per[0], per[1] = 0, i * size

            def turned(size, turns):
                assert per[0] == size, (per[0], size)
                steps[0] += size * turns
                per[0], per[1] = 0, 0

            for i in range(PAIRS):
                dve.wait_ge(x_loaded[0], i * 16 + 16)
                dve.wait_ge(x_loaded[1], i * 16 + 16)
                for k in range(2 * Q):
                    last = v.bn_stats(stats[:, i * (2 * Q) + k, :], xtok[:, i * 2 + k // Q, P * (k % Q):P * (k % Q) + P])
                link(last)
                for k in range(2 * Q):
                    last = v.bn_aggr(mv[:, i * (2 * Q) + k, :], stats[:, i * (2 * Q) + k, :])
                last.then_inc(var_ready, 1)

            with dve.Fori(0, PAIRS) as i:
                dve.wait_ge(rstd_ready, i + 1)
                dve.wait_ge(var_ready, i + 1)
                for k in range(2 * Q):
                    f = i * (2 * Q) + k
                    t = xtok[:, i * 2 + k // Q, P * (k % Q):P * (k % Q) + P]
                    last = v.tensor_scalar(t, t, mv[:, f, 0:1], rs1[:, bass.ds(f, 1)], ALU.subtract, ALU.mult)
                last.then_inc(xn_ready, 1)

            dve.wait_ge(w_loaded, N_LOADS)
            v.tensor_scalar(om[:, :], par[:, :], -1.0, 1.0, ALU.mult, ALU.add)
            link(v.memset(wrow[:, :], 1.0))
            v.tensor_scalar(wrow[:, :], wrow[:, :], col["time_decay"], None, ALU.mult)
            v.tensor_tensor(wtm[:, :], wtm[:, :], mixrow[:, :], ALU.mult)
            link(v.tensor_tensor(wcm[:, :].rearrange("p (j c) -> p j c", j=NJ), wcm[:, :].rearrange("p (j c) -> p j c", j=NJ),
                                 cmkrow[:, :].unsqueeze(1).broadcast_to([P, NJ, C]), ALU.mult))
            dve.sem_inc(weights_ready, 1)
            dve.wait_ge(consts_ready, 1)

            def mix(dst, b, name, psum, psum_sem, ready, first=0):
                dve.wait_ge(psum_sem, b + (1 + first))
                v.scalar_tensor_tensor(dst[:, b, :], xT[:, b, 0:T], omc[name], psum[:, :],
                                       ALU.mult, ALU.add).then_inc(ready, 1)

            def coefficients(i, ready):
                d = kd[:, bass.ts(i, 2), :]
                v.tensor_scalar(ca[:, bass.ts(i, 2), :], d, col["time_decay"], 0.0, ALU.subtract, ALU.max)
                v.tensor_scalar(cb[:, bass.ts(i, 2), :], d, col["time_decay"], 0.0, ALU.subtract, ALU.min)\
                    .then_inc(ready, 1)

            with dve.Fori(0, PAIRS) as i:
                turn(i, 1)
                for s in range(2):
                    b = i * 2 + s
                    mix(kd, b, "tmk", mm[0], k_psum, k_ready)
                    mix(vb, b, "tmv", mm[1], v_psum, v_ready)
                    mix(rb, b, "tmr", mv_ps, r_psum, r_ready, 2)
                    dve.wait_ge(k_ready, b + 1)
                    v.tensor_tensor_scan(st[:, b, 1:T + 1], wrow[:, :], kd[:, b, :], NEG_INF,
                                         ALU.add, ALU.max).then_inc(m_ready, 1)
                dve.wait_ge(m_ready, i * 2 + 2)
                link(v.tensor_tensor(kd[:, bass.ts(i, 2), :], kd[:, bass.ts(i, 2), :], st[:, bass.ts(i, 2), 0:T], ALU.subtract))
                coefficients(i, ab_ready)
            turned(1, PAIRS)

            dve.wait_ge(logits_psum, B)
            link(v.tensor_reduce(rmax[:, :], lg, AX.X, ALU.max))
            v.tensor_tensor(prob[:, :, :], lg, rmax[:, :].unsqueeze(2).broadcast_to([P, NF, E]), ALU.subtract)\
                .then_inc(lmax_ready, 1)
            dve.wait_ge(lexp_ready, 1)
            link(v.tensor_reduce(rmax[:, :], prob[:, :, :], AX.X, ALU.add))
            link(v.reciprocal(rmax[:, :], rmax[:, :]))
            v.tensor_tensor(prob[:, :, :], prob[:, :, :], rmax[:, :].unsqueeze(2).broadcast_to([P, NF, E]), ALU.mult)\
                .then_inc(prob_ready, 1)
            dve.wait_ge(prob_ready, 1)
            v.tensor_scalar(pcl[:, :, :], prob[:, :, :], TINY, None, ALU.max)
            v.memset(thr[:, :], TINY)
            link(v.memset(cand[:, :], TINY * exp_factors[0]))
            p_e = pcl[:, :, :].rearrange("p f e -> p e f")

            def reach():
                v.tensor_tensor(cmp[:, :, :], cand[:, :].unsqueeze(2).broadcast_to([P, E, NF]), p_e, ALU.is_le)\
                    .then_inc(cmp_ready, 1)

            reach()

            def search(n, nxt, mantissa):
                dve.wait_ge(count_psum, n + 1)
                link(v.tensor_reduce(cnt[:, :], cps, AX.X, ALU.add))
                link(v.scalar_tensor_tensor(cand[:, :], cnt[:, :], KTOP - 0.5, cand[:, :], ALU.is_ge, ALU.mult))
                link(v.tensor_tensor(thr[:, :], thr[:, :], cand[:, :], ALU.max))
                if mantissa:
                    link(v.scalar_tensor_tensor(cand[:, :], step[:, :], factor[:, bass.ds(nxt, 1)], thr[:, :],
                                                ALU.mult, ALU.add))
                else:
                    link(v.tensor_scalar(cand[:, :], thr[:, :], factor[:, bass.ds(nxt, 1)], None, ALU.mult))
                reach()

            link(v.memset(st[:, :, 0:1], 1.0))
            with dve.Fori(0, PAIRS) as i:
                turn(i, 8)
                search(i * 2, i * 2 + 1, False)
                dve.wait_ge(abexp_ready, i + 1)
                for s in range(2):
                    b = i * 2 + s
                    v.tensor_tensor_scan(st[:, b, 1:T + 1], ca[:, b, :], cb[:, b, :], 1.0, ALU.mult, ALU.add)\
                        .then_inc(s_ready, 1)
                search(i * 2 + 1, i * 2 + 2, False)
            turned(8, PAIRS)
            link(v.tensor_copy(step[:, :], thr[:, :]))

            m0 = len(exp_factors)
            with dve.Fori(0, PAIRS) as i:
                turn(i, 13)
                for k in range(3):
                    search(i * 3 + (EXP_STEPS + k), i * 3 + (m0 + k), True)
                    if k == 0:
                        dve.wait_ge(lns_ready, i + 1)
                        link(v.tensor_tensor(kd[:, bass.ts(i, 2), :], kd[:, bass.ts(i, 2), :],
                                             st[:, bass.ts(i, 2), 0:T], ALU.subtract))
                        coefficients(i, e_ready)
            turned(13, PAIRS)

            dve.wait_ge(lns_ready, PAIRS)
            link(v.memset(st[:, :, 0:1], 0.0))
            with dve.Fori(0, PAIRS) as i:
                turn(i, 13)
                for k in range(3):
                    search(i * 3 + (EXP_STEPS + 3 * PAIRS + k), i * 3 + (m0 + 3 * PAIRS + k), True)
                    if k == 0:
                        dve.wait_ge(eexp_ready, i + 1)
                        link(v.tensor_tensor(cb[:, bass.ts(i, 2), :], cb[:, bass.ts(i, 2), :], vb[:, bass.ts(i, 2), :], ALU.mult))
                    else:
                        b = i * 2 + (k - 1)
                        v.tensor_tensor_scan(st[:, b, 1:T + 1], ca[:, b, :], cb[:, b, :], 0.0, ALU.mult, ALU.add)\
                            .then_inc(aa_ready, 1)
            turned(13, PAIRS)

            def per_e(t):
                return t[:, :].rearrange("p (e f) -> p e f", e=E)

            thr_b = thr[:, :].unsqueeze(2).broadcast_to([P, E, NF])
            v.tensor_tensor(gt[:, :, :], p_e, thr_b, ALU.is_gt)
            link(v.tensor_tensor(eq[:, :, :], p_e, thr_b, ALU.is_equal))
            nc_ = nc
            with nc_.allow_low_precision(reason="counts up to 32 are exact in bfloat16"):
                v.tensor_reduce(gtc[:, :], gt[:, :, :], AX.X, ALU.add)
                v.tensor_reduce(rows4[:, :], eq[:, :, :].rearrange("p e (b q) -> p (e b) q", q=Q), AX.X, ALU.add)\
                    .then_inc(ties_ready, 1)
            eq_flat = eq[:, :, :].rearrange("p e f -> p (e f)")
            gt_flat = gt[:, :, :].rearrange("p e f -> p (e f)")
            link(v.tensor_tensor_scan(sc[:, :], restart_q[:, :], eq_flat, 0.0, ALU.mult, ALU.add))
            link(v.tensor_tensor(sc[:, :], sc[:, :], eq_flat, ALU.subtract))
            dve.wait_ge(ties_psum, 1)
            pre, tot, gtt = tie_ps[:, 0:E * B], tie_ps[:, E * B:2 * E * B], tie_ps[:, 2 * E * B:2 * E * B + E]
            link(v.tensor_tensor_scan(bex[:, :], restart_b[:, :], tot, 0.0, ALU.mult, ALU.add))
            link(v.tensor_tensor(bex[:, :], bex[:, :], tot, ALU.subtract))
            link(v.tensor_tensor(bex[:, :], bex[:, :], pre, ALU.add))
            v.tensor_scalar(need[:, :], gtt, -1.0, float(KTOP), ALU.mult, ALU.add)
            link(v.tensor_tensor(sc[:, :].rearrange("p (n q) -> p n q", q=Q), sc[:, :].rearrange("p (n q) -> p n q", q=Q),
                                 bex[:, :].unsqueeze(2).broadcast_to([P, E * B, Q]), ALU.add))
            link(v.tensor_tensor(per_e(sc), per_e(sc), need[:, :].unsqueeze(2).broadcast_to([P, E, NF]), ALU.is_lt))
            link(v.tensor_tensor(sc[:, :], sc[:, :], eq_flat, ALU.mult))
            link(v.tensor_tensor(gt_flat, gt_flat, sc[:, :], ALU.add))
            link(v.tensor_tensor_scan(sd[:, :], restart_e[:, :], gt_flat, 0.0, ALU.mult, ALU.add))
            v.tensor_copy(selc[:, :], per_e(sd)[:, :, NF - 1]).then_inc(selc_ready, 1)
            link(v.tensor_scalar(sc[:, :], gt_flat, -float(KTOP + 1), float(KTOP), ALU.mult, ALU.add))
            link(v.tensor_tensor(sd[:, :], sd[:, :], sc[:, :], ALU.add))
            dve.wait_ge(selc_psum, 1)
            sel_pre = tie_ps[:, 2 * E * B + E:2 * E * B + 2 * E]
            link(v.tensor_tensor(per_e(slot), per_e(sd), sel_pre.unsqueeze(2).broadcast_to([P, E, NF]), ALU.add))
            v.tensor_scalar(slot_hi[:, :], slot[:, :], 5, None, ALU.arith_shift_right)
            link(v.tensor_scalar(slot_lo[:, :], slot[:, :], LO - 1, None, ALU.bitwise_and))
            v.tensor_copy(hi16[:, :], slot_hi[:, :])
            link(v.tensor_copy(lo16[:, :], slot_lo[:, :]))
            for h in range(HI):
                last = v.tensor_scalar(oh_hi[:, 1, h, :], hi16[:, :], float(h), None, ALU.is_equal)
            link(last)
            bc = [P, HI, E * NF]
            v.tensor_tensor(oh_hi[:, 0, :, :], oh_hi[:, 1, :, :], tok_lo[:, :].unsqueeze(1).broadcast_to(bc), ALU.mult)
            v.tensor_tensor(oh_hi[:, 1, :, :], oh_hi[:, 1, :, :], tok_hi[:, :].unsqueeze(1).broadcast_to(bc), ALU.mult)
            dve.wait_ge(rows_stored, 16 * 2 * B)
            for l in range(LO):
                last = v.tensor_scalar(oh_lo[:, l, :], lo16[:, :], float(l), None, ALU.is_equal)
            last.then_inc(onehot_ready, 1)
            dve.wait_ge(idx_psum, 1)
            f_v = idxf[:, :].rearrange("l (e h) -> l e h", e=E)
            link(v.tensor_copy(f_v, idx_ps[:, :, 0, :]))
            link(v.tensor_tensor(f_v, f_v, idx_ps[:, :, 1, :], ALU.add))
            f_g = idxf[:, :].rearrange("l (n j) -> l n j", j=P // LO)
            for j in range(P // LO):
                last = v.tensor_copy(idx[LO * j:LO * j + LO, :], f_g[:, :, j])
            last.then_inc(idx_ready, 1)

            with dve.Fori(0, PAIRS) as i:
                turn(i, 5)
                pr = bass.ts(i, 2)
                dve.wait_ge(gates_ready, i + 1)
                dve.wait_ge(aa_ready, i * 2 + 2)
                y, aa, x1 = ca[:, pr, :], st[:, pr, 0:T], xT[:, pr, 1:T + 1]
                link(v.tensor_tensor(y, vb[:, pr, :], aa, ALU.subtract))
                link(v.tensor_tensor(y, y, kd[:, pr, :], ALU.mult))
                link(v.tensor_tensor(y, y, aa, ALU.add))
                link(v.tensor_tensor(y, y, rb[:, pr, :], ALU.mult))
                link(v.tensor_tensor(x1, y, x1, ALU.add))
                v.tensor_copy(xT[:, pr, 0:1], xT[:, pr, T:T + 1]).then_inc(x1_ready, 1)
            turned(5, PAIRS)

            for i in range(PAIRS):
                dve.wait_ge(x1tok_ready, i * 2 + 2)
                for k in range(2 * Q):
                    last = v.bn_stats(stats[:, i * (2 * Q) + k, :], vb[:, i * 2 + k // Q, P * (k % Q):P * (k % Q) + P])
                link(last)
                for k in range(2 * Q):
                    last = v.bn_aggr(mv[:, i * (2 * Q) + k, :], stats[:, i * (2 * Q) + k, :])
                last.then_inc(var2_ready, 1)
            with dve.Fori(0, PAIRS) as i:
                dve.wait_ge(rstd2_ready, i + 1)
                dve.wait_ge(var2_ready, i + 1)
                for k in range(2 * Q):
                    f = i * (2 * Q) + k
                    t = vb[:, i * 2 + k // Q, P * (k % Q):P * (k % Q) + P]
                    last = v.tensor_scalar(t, t, mv[:, f, 0:1], rs2[:, bass.ds(f, 1)], ALU.subtract, ALU.mult)
                last.then_inc(xn2_ready, 1)

            with dve.Fori(0, PAIRS) as i:
                turn(i, 1)
                pr = bass.ts(i, 2)
                xp = xT[:, pr, 0:T]
                v.tensor_scalar(kd[:, pr, :], xp, omc["cmk"], None, ALU.mult)
                link(v.tensor_scalar(ca[:, pr, :], xp, omc["cmr"], None, ALU.mult))
                dve.wait_ge(xn2T_ready, i * 2 + 2)
                v.scalar_tensor_tensor(cb[:, pr, :], rb[:, pr, :], col["cmr"], ca[:, pr, :], ALU.mult, ALU.add)\
                    .then_inc(z_ready, 1)
            turned(1, PAIRS)

            def hidden(b):
                dve.wait_ge(vv_psum, b + 1)
                for j in range(NJ):
                    dve.wait_ge(kk_psum, b * NJ + (j + 1))
                    v.tensor_tensor(rel[:, j, :], mm[j % 2][:, :], kd[:, b, :], ALU.add).then_inc(kk_ready, 1)

            def x2(b):
                dve.wait_ge(vv_psum, b + 2)
                link(v.tensor_tensor(st[:, b, 0:T], mv_ps[:, :], cb[:, b, :], ALU.mult))
                v.tensor_tensor(st[:, b, 0:T], st[:, b, 0:T], xT[:, b, 1:T + 1], ALU.add).then_inc(x2_ready, 1)

            def result(b, i, s):
                dve.wait_ge(x2tok_psum, b + 1)
                dve.wait_ge(base_loaded[s], i * 16 + 16)
                v.tensor_tensor(yb[:, s, :], tp[s][:, :], yb[:, s, :], ALU.add).then_inc(res_ready, 1)

            with dve.Fori(0, PAIRS) as i:
                turn(i, 2)
                dve.wait_ge(rr_ready, i + 1)
                hidden(i * 2)
                x2(i * 2)
                hidden(i * 2 + 1)
                result(i * 2, i, 0)
                x2(i * 2 + 1)
                result(i * 2 + 1, i, 1)
            turned(2, PAIRS)

        @block.tensor
        def _(pe):
            t = nc.tensor

            def wait(s, value):
                if value > 0:
                    pe.wait_ge(s, value)

            pe.sem_inc(r_psum, 2)
            pe.sem_inc(vv_psum, 1)
            pe.wait_ge(consts_ready, 1)

            def kvr(b):
                wait(hT_ready, b + 1)
                for dst, n, ready, done in ((mm[0], 0, k_ready, k_psum), (mm[1], 1, v_ready, v_psum),
                                            (mv_ps, 2, r_ready, r_psum)):
                    wait(ready, b)
                    t.matmul(dst[:, :], wtm[:, C * n:C * n + C], hT[:, b % 2, :], start=True, stop=True).then_inc(done, 1)

            for b in range(B):
                wait(xn_ready, b // 2 + 1)
                wait(xT_ready, b)
                for q in range(Q):
                    last = t.transpose(tp[0][:, q:T:Q], xtok[:, b, P * q:P * q + P], ident[:, :])
                last.then_inc(xT_psum, 1)
                wait(h_ready, b // 2 + 1)
                wait(hT_ready, b)
                for q in range(Q):
                    last = t.transpose(tp[1][:, q:T:Q], htok[:, b, P * q:P * q + P], ident[:, :])
                last.then_inc(hT_psum, 1)
                if b == 0:
                    pe.wait_ge(weights_ready, 1)
                wait(xT_ready, b + 1)
                for q in range(Q):
                    t.matmul(lg[:, Q * b + q, :], xT[:, b, 1 + q:T + 1:Q], wr[:, :], start=True, stop=False)
                    last = t.matmul(lg[:, Q * b + q, :], onerow[0:1, :], brr[0:1, :], start=False, stop=True)
                last.then_inc(logits_psum, 1)
                kvr(b)

            for n in range(1 + EXP_STEPS + MAN_STEPS):
                pe.wait_ge(cmp_ready, n + 1)
                t.matmul(small[:, NF * E:2 * NF * E], ones[:, :], cmp[:, :, :].rearrange("p e f -> p (e f)"),
                         start=True, stop=True).then_inc(count_psum, 1)

            pe.wait_ge(ties_ready, 1)
            t.matmul(tie_ps[:, 0:E * B], upper[:, :], rows4[:, :], start=True, stop=True)
            t.matmul(tie_ps[:, E * B:2 * E * B], ones[:, :], rows4[:, :], start=True, stop=True)
            t.matmul(tie_ps[:, 2 * E * B:2 * E * B + E], ones[:, :], gtc[:, :], start=True, stop=True)\
                .then_inc(ties_psum, 1)
            pe.wait_ge(selc_ready, 1)
            t.matmul(tie_ps[:, 2 * E * B + E:2 * E * B + 2 * E], upper[:, :], selc[:, :], start=True, stop=True)\
                .then_inc(selc_psum, 1)

            pe.wait_ge(onehot_ready, 1)
            for e in range(E):
                for f in range(NF):
                    last = t.matmul(idx_ps[:, e, :, :], oh_lo[:, :, e * NF + f], oh_hi[:, :, :, e * NF + f],
                                    start=(f == 0), stop=(f == NF - 1))
            last.then_inc(idx_psum, 1)

            def expert(e):
                s = e % 2
                pe.wait_ge(gathered[s], 16 * NG * (e // 2 + 1))
                wait(mid_ready, len(FJ) * e)
                wait(yo_ready, e + 2)
                for k in range(NG):
                    last = t.transpose(moe[s][:, P * k:P * k + P], gath[:, s, k, 0:C], ident[:, :])
                last.then_inc(gT_psum, 1)
                wait(xg_ready, e + 1)
                for j, fj in enumerate(FJ):
                    if j == 2:
                        wait(mid_ready, len(FJ) * e + 1)
                    t.matmul(moe[(s + 1 + j) % 2][0:fj, :], wup[:, e // EG, P * j:P * j + fj], xg[:, s, :],
                             start=True, stop=True).then_inc(up_psum, 1)
                wait(mid_ready, len(FJ) * (e + 1))
                for k in range(NG):
                    for j, fj in enumerate(FJ):
                        rows = fj + (j == len(FJ) - 1)
                        last = t.matmul(moe[s][:, C * k:C * k + C], mid[0:rows, s, j, P * k:P * k + P],
                                        wdn[0:rows, e, j, :], start=(j == 0), stop=(j == len(FJ) - 1))
                last.then_inc(down_psum, 1)

            for b in range(B):
                pe.wait_ge(x1_ready, b // 2 + 1)
                wait(x1tok_ready, b - 1)
                for q in range(Q):
                    last = t.transpose(tp[b % 2][:, P * q:P * q + P], xT[:, b, 1 + q:T + 1:Q], ident[:, :])
                last.then_inc(x1tok_psum, 1)
                expert(b)
            for b in range(B):
                pe.wait_ge(xn2_ready, b // 2 + 1)
                wait(x1tok_ready, B)
                wait(xn2T_ready, b - 1)
                for q in range(Q):
                    last = t.transpose(tp[b % 2][:, q:T:Q], vb[:, b, P * q:P * q + P], ident[:, :])
                last.then_inc(xn2T_psum, 1)

            def back(b):
                pe.wait_ge(x2_ready, b + 1)
                wait(res_ready, b - 1)
                for q in range(Q):
                    last = t.transpose(tp[b % 2][:, P * q:P * q + P], st[:, b, q:T:Q], ident[:, :])
                last.then_inc(x2tok_psum, 1)

            wait(xn2T_ready, B)
            for b in range(B):
                def up(j):
                    wait(kk_ready, NJ * b + j - 1)
                    t.matmul(mm[j % 2][:, :], wcm[:, C * j:C * j + C], rb[:, b, :], start=True, stop=True).then_inc(kk_psum, 1)

                def down(j):
                    wait(sq_ready, NJ * b + j + 1)
                    if j == 0:
                        wait(x2_ready, b)
                    return t.matmul(mv_ps[:, :], wcp[:, j, :], rel[:, j, :], start=(j == 0), stop=(j == NJ - 1))

                up(0)
                up(1)
                if b:
                    back(b - 1)
                for j in range(NJ):
                    last = down(j)
                    if j + 2 < NJ:
                        up(j + 2)
                last.then_inc(vv_psum, 1)
            back(B - 1)


_INS = ["attn_x", "attn_time_decay", "attn_time_first", "attn_W_tm", "attn_g1", "attn_b1", "attn_tmk", "attn_tmv",
        "attn_tmr", "attn_W_cm", "attn_W_cp", "attn_g2", "attn_b2", "attn_cmk", "attn_cmr", "ffn_Wr", "ffn_br",
        "ffn_W_up", "ffn_b_up", "ffn_W_down", "ffn_b_down"]


def kernel(**inputs):
    import numpy as _np
    import concourse.bacc as _bacc
    from concourse import mybir as _mybir
    from concourse.bass_utils import run_bass_kernel_spmd as _run

    nc = _bacc.Bacc("TRN2", target_bir_lowering=False, num_devices=1)
    arrays, args = {}, []
    for name in _INS:
        a = _np.ascontiguousarray(inputs["L0_" + name])
        if name in ("attn_tmk", "attn_tmv", "attn_tmr", "attn_cmk", "attn_cmr"):
            a = a.reshape(-1)
        arrays[f"in_{name}"] = a
        args.append(nc.dram_tensor(f"in_{name}", a.shape, _mybir.dt.from_np(a.dtype), kind="ExternalInput").ap())
    shape = inputs["L0_attn_x"].shape
    args.append(nc.dram_tensor("out_0", shape, _mybir.dt.float32, kind="ExternalOutput").ap())
    rwkv_plus_expert_choice(nc, *args)
    r = _run(nc, [arrays], core_ids=[0])
    return r.results[0]["out_0"]
```

```python
from contextlib import ExitStack

import concourse.bass as bass
from concourse import mybir

ALU = mybir.AluOpType
ACT = mybir.ActivationFunctionType
F32 = mybir.dt.float32
F16 = mybir.dt.float16
BF16 = mybir.dt.bfloat16
I32 = mybir.dt.int32
U32 = mybir.dt.uint32
AX = mybir.AxisListType

PARAMS = ["time_decay", "time_first", "g1", "b1", "tmk", "tmv", "tmr", "g2", "b2", "cmk", "cmr"]
MIXES = ["tmk", "tmv", "tmr", "cmk"]


def rwkv_plus_expert_choice(nc, x, chan_cols, chan_rows, W_tm, W_cm, W_cp, Wr, br, W_up, b_up_t, W_down, b_down, out):
    B, T, C = x.shape
    E = Wr.shape[1]
    NGRP, _, F = W_up.shape
    EG = E // NGRP
    P = 128
    assert C == P and T == 4 * P and E == B and EG == 2
    Q = T // P
    NTOK = B * T
    NF = B * Q
    KTOP = NTOK // E
    NG = KTOP // P
    FJ = [min(P, F - P * j) for j in range((F + P - 1) // P)]
    NJ = W_cm.shape[1] // C
    TP = T + 2
    ROW = C + E
    PAIRS = B // 2
    LN_EPS, WKV_EPS, NEG_INF = 1e-5, 1e-8, -1e38
    LO, HI = 32, KTOP // 32

    TINY, SCALE = 2.0 ** -126, 2.0 ** 100
    EXP_STEPS = (64, 32, 16, 8, 4, 2, 1)
    MAN_BITS = 23
    TURN_STEPS = 7
    assert len(EXP_STEPS) == 7 and 1 + TURN_STEPS * (PAIRS - 1) + 1 == MAN_BITS
    CH = P // E
    W = NTOK // CH

    xn_rows = nc.dram_tensor("xn_rows", [NTOK, ROW], F32, kind="Internal").ap()
    y_base = nc.dram_tensor("y_base", [NTOK, C], F32, kind="Internal").ap()
    x_v = x.rearrange("b (q p) c -> b p q c", q=Q)
    out_v = out.rearrange("b (q p) c -> b p q c", q=Q)
    base_v = y_base.rearrange("(b q p) c -> b p q c", p=P, q=Q)
    rows_v = xn_rows.rearrange("(f p) c -> p f c", p=P)

    ctx = ExitStack()
    with ctx:
        def sb(name, shape, dt=F32):
            return ctx.enter_context(nc.sbuf_tensor(name, shape, dt))

        def pb(name, shape, dt=F32):
            return ctx.enter_context(nc.psum_tensor(name, shape, dt))

        def sem(name):
            return ctx.enter_context(nc.semaphore(name))

        xtok = sb("xtok", [P, B, T])
        htok = sb("htok", [P, B, T])
        xT = sb("xT", [P, B, TP])
        kd = sb("kd", [P, B, T])
        st = sb("st", [P, B, TP])
        vb = sb("vb", [P, B, T])
        rb = sb("rb", [P, B, T])
        ca = sb("ca", [P, B, T])
        cb = sb("cb", [P, B, T])
        rel = vb[:, :, :].rearrange("p (s j) t -> p s j t", s=2)

        par = sb("par", [P, len(PARAMS)])
        om = sb("om", [P, len(PARAMS)])
        negw = sb("negw", [P, 1])
        col = {n: par[:, i:i + 1] for i, n in enumerate(PARAMS)}
        omc = {n: om[:, i:i + 1] for i, n in enumerate(PARAMS)}
        wrow = sb("wrow", [P, T])
        mixrow = sb("mixrow", [P, len(MIXES), C])
        wtm = sb("wtm", [P, 3 * C])
        wcm = sb("wcm", [P, NJ * C])
        wcp = sb("wcp", [P, NJ, C])
        wr = sb("wr", [P, E])
        brr = sb("brr", [P, E])
        wup = sb("wup", [P, NGRP, F])
        bup = sb("bup", [P, NGRP, len(FJ)])
        wdn = sb("wdn", [P, E, len(FJ), C])
        ident = sb("ident", [P, P])
        same = sb("same", [P, P], BF16)
        earlier = sb("earlier", [P, P], BF16)
        weps = sb("weps", [P, 1])

        stats = sb("stats", [P, NF, 6])
        mv = sb("mv", [P, NF, 2])
        rs = sb("rs", [P, 2, NF])
        nt = sb("nt", [P, 2, NF])
        va = sb("va", [P, 2, NF])
        nb = sb("nb", [P, NF])

        prob = sb("prob", [P, NF, E])
        pcl = sb("pcl", [P, 2, E, CH])
        rmax = sb("rmax", [P, NF])
        pE = sb("pE", [P, W])
        hit = sb("hit", [P, W], BF16)
        cand = sb("cand", [P, 1])
        delta = sb("delta", [P, 1])
        ok = sb("ok", [P, 1])
        cnt = sb("cnt", [P, 1], BF16)
        gtc = sb("gtc", [P, 1], BF16)
        eqc = sb("eqc", [P, 1], BF16)
        selc = sb("selc", [P, 1], BF16)
        need = sb("need", [P, 1])
        gt = sb("gt", [P, W])
        eq = sb("eq", [P, W])
        rank = sb("rank", [P, W])
        onesw = sb("onesw", [P, W])
        slot = sb("slot", [P, 2 * P], I32)
        slot_hi = sb("slot_hi", [P, 2 * P], I32)
        slot_lo = sb("slot_lo", [P, 2 * P], I32)
        hi16 = sb("hi16", [P, 2 * P], F16)
        lo16 = sb("lo16", [P, 2 * P], F16)
        centred = sb("centred", [P, 2 * P], F16)
        assert NTOK // 2 <= 2048
        oh_lo = xtok[:, :, :].rearrange("p b t -> p (b t)").bitcast(F16).rearrange("p (l n) -> p l n", l=LO)
        oh_hi = htok[:, :, :].rearrange("p b t -> p (b t)").bitcast(F16)[:, 0:HI * 2 * P]\
            .rearrange("p (h n) -> p h n", h=HI)
        idxf = sb("idxf", [LO, E * HI])
        idx = sb("idx", [P, E * NG], U32)

        gath = sb("gath", [P, E, NG, ROW])
        xt_flat = xtok[:, :, :].rearrange("p b t -> p (b t)")
        ht_flat = htok[:, :, :].rearrange("p b t -> p (b t)")
        n_x = 2 * KTOP
        xg = xt_flat[:, 0:n_x].rearrange("p (s n) -> p s n", s=2)
        yo = xt_flat[:, n_x:2 * n_x].rearrange("p (s k c) -> p s k c", s=2, k=NG)
        mid = ht_flat[:, 0:2 * len(FJ) * KTOP].rearrange("p (s j n) -> p s j n", s=2, j=len(FJ))

        tp = [pb("tp0", [P, T]), pb("tp1", [P, T])]
        mm = [pb("mm0", [P, T]), pb("mm1", [P, T])]
        mv_ps = pb("mv_ps", [P, T])
        moe = [pb("moe0", [P, T]), pb("moe1", [P, T])]
        small = pb("small", [P, T])
        lg = small[:, 0:NF * E].rearrange("p (f e) -> p f e", e=E)
        cps = small[:, NF * E:NF * E + 1]
        sel_ps = small[:, NF * E + 8:NF * E + 16]
        pt_ps = small[:, 0:W]
        sl_ps = tp[1]
        idx_ps = tp[0][0:LO, 0:E * HI].rearrange("l (e h) -> l e h", e=E)
        kvr_ps = [(mm[0], mm[1], mv_ps), (moe[0], moe[1], tp[1])]
        kk_ps = [mm[0], mm[1], small]

        x_loaded = [sem(f"x_loaded{b}") for b in range(B)]
        w_loaded = sem("w_loaded")
        late_loaded = sem("late_loaded")
        base_copied = sem("base_copied")
        pool_step = sem("pool_step")
        consts_ready = sem("consts_ready")
        dve_step = sem("dve_step")
        act_step = sem("act_step")
        weights_ready = sem("weights_ready")
        mv_ready = sem("mv_ready")
        rs_ready = sem("rs_ready")
        xn_ready = sem("xn_ready")
        h_ready = sem("h_ready")
        rows_stored = sem("rows_stored")
        probs_stored = sem("probs_stored")
        xT_psum = sem("xT_psum")
        hT_psum = sem("hT_psum")
        xT_ready = sem("xT_ready")
        hT_ready = sem("hT_ready")
        logits_psum = sem("logits_psum")
        k_psum = sem("k_psum")
        v_psum = sem("v_psum")
        r_psum = sem("r_psum")
        k_ready = sem("k_ready")
        v_ready = sem("v_ready")
        r_ready = sem("r_ready")
        r_copied = sem("r_copied")
        m_ready = sem("m_ready")
        ab_ready = sem("ab_ready")
        relu_ready = sem("relu_ready")
        abexp_ready = sem("abexp_ready")
        s_ready = sem("s_ready")
        lns_ready = sem("lns_ready")
        e_ready = sem("e_ready")
        eexp_ready = sem("eexp_ready")
        aa_ready = sem("aa_ready")
        gates_ready = sem("gates_ready")
        x1_ready = sem("x1_ready")
        xp_ready = sem("xp_ready")
        lmax_ready = sem("lmax_ready")
        lexp_ready = sem("lexp_ready")
        prob_ready = sem("prob_ready")
        pcl_ready = sem("pcl_ready")
        pE_psum = sem("pE_psum")
        pE_ready = sem("pE_ready")
        cnt_ready = sem("cnt_ready")
        count_psum = sem("count_psum")
        ties_ready = sem("ties_ready")
        ties_psum = sem("ties_psum")
        selc_ready = sem("selc_ready")
        selc_psum = sem("selc_psum")
        slot_ready = sem("slot_ready")
        slot_psum = sem("slot_psum")
        onehot_ready = sem("onehot_ready")
        idx_psum = sem("idx_psum")
        idx_ready = sem("idx_ready")
        gathered = [sem(f"gathered{e}") for e in range(E)]
        gT_psum = sem("gT_psum")
        xg_ready = sem("xg_ready")
        up_psum = sem("up_psum")
        mid_ready = sem("mid_ready")
        mid_ones = sem("mid_ones")
        down_psum = sem("down_psum")
        yo_ready = sem("yo_ready")
        scattered = [sem("scattered0"), sem("scattered1")]
        yo_added = sem("yo_added")
        tp_filled = sem("tp_filled")
        tp_copied = sem("tp_copied")
        xn2_ready = sem("xn2_ready")
        z_ready = sem("z_ready")
        rr_ready = sem("rr_ready")
        kk_psum = sem("kk_psum")
        kk_ready = sem("kk_ready")
        sq_ready = sem("sq_ready")
        vv_psum = sem("vv_psum")
        x2_ready = sem("x2_ready")
        base_loaded = [sem("base_loaded0"), sem("base_loaded1")]
        res_ready = sem("res_ready")
        out_stored = sem("out_stored")

        loads = [(par[:, :], chan_cols), (wtm[:, :], W_tm),
                 (mixrow[:, :, :], chan_rows.rearrange("(o n) c -> o n c", o=1).broadcast_to([P, len(MIXES), C])),
                 (wr[:, :], Wr), (brr[:, :], br.rearrange("(o e) -> o e", o=1).broadcast_to([P, E])),
                 (wcm[:, :], W_cm)]
        late = [(wcp[:, :, :], W_cp.rearrange("(j k) c -> k j c", j=NJ)),
                (wup[:, :, :], W_up.rearrange("g h f -> h g f"))]
        for j, fj in enumerate(FJ):
            late.append((bup[0:fj, :, j], b_up_t[P * j:P * j + fj, :]))
            late.append((wdn[0:fj, :, j, :], W_down[:, P * j:P * j + fj, :].rearrange("e f c -> f e c")))
        late.append((wdn[FJ[-1]:FJ[-1] + 1, :, len(FJ) - 1, :], b_down.rearrange("(o e) c -> o e c", o=1)))
        N_LOADS, N_LATE = 16 * len(loads), 16 * len(late)

        parts = [(2 * i, 2 * i + 1) for i in range(PAIRS)]
        rs_part = {b: n + 1 for n, mine in enumerate(parts) for b in mine}

        ORDER = [("ln", 0), ("ln", 1), ("ln", 2), ("ln", 3), ("eexp", 0), ("eexp", 1), ("eexp", 2), ("eexp", 3),
                 ("gates", 0), ("gates", 1), ("gates", 2), ("gates", 3),
                 ("expert", 0), ("expert", 1), ("x1tok", 0), ("expert", 2), ("x1tok", 1), ("xn2T", 0), ("rr", 0),
                 ("expert", 3), ("x1tok", 2), ("up", 0), ("squares", 0), ("xn2T", 1), ("rr", 1), ("x1tok", 3),
                 ("up", 1), ("squares", 1), ("down", 0), ("expert", 4), ("up", 2), ("squares", 2), ("down", 1), ("x2tok", 0),
                 ("xn2T", 2), ("rr", 2),
                 ("up", 3), ("squares", 3), ("down", 2), ("x2tok", 1), ("expert", 5), ("up", 4), ("squares", 4),
                 ("down", 3), ("x2tok", 2), ("xn2T", 3), ("rr", 3), ("up", 5), ("squares", 5), ("down", 4), ("x2tok", 3),
                 ("expert", 6), ("up", 6), ("squares", 6), ("down", 5), ("x2tok", 4), ("expert", 7),
                 ("up", 7), ("squares", 7), ("down", 6), ("x2tok", 5), ("down", 7), ("x2tok", 6), ("x2tok", 7)]
        tp_turn = {}
        for kind, n in ORDER:
            for b in (2 * n, 2 * n + 1) if kind in ("x1tok", "xn2T") else (n,) if kind == "x2tok" else ():
                tp_turn[kind, b] = len(tp_turn)

        def position(b):
            return (0 if b < 2 else len(EXP_STEPS) + 1 + TURN_STEPS * (b // 2 - 1)) + 3 * (b % 2)

        def rsqrt(engine, link, k, part):
            y, t, u = rs[:, 0:k, part], nt[:, 0:k, part], va[:, 0:k, part]
            link(engine.tensor_scalar(y.bitcast(I32), u.bitcast(I32), -0.5, float(0x5F3759DF), ALU.mult, ALU.add))
            for _ in range(3):
                link(engine.tensor_tensor(t, y, y, ALU.mult))
                link(engine.tensor_tensor(t, t, u, ALU.mult))
                link(engine.tensor_scalar(t, t, -0.5, 1.5, ALU.mult, ALU.add))
                link(engine.tensor_tensor(y, y, t, ALU.mult))

        block = ctx.enter_context(nc.Block())

        @block.sync
        def _(sp):
            def tiles(t, b):
                return t[:, b, :].rearrange("p (q c) -> p q c", q=Q)

            for b in range(B):
                sp.dma_start(tiles(xtok, b), x_v[b, :, :, :]).then_inc(x_loaded[b], 16)
            with nc.allow_non_contiguous_dma(reason="a few hundred bias values"):
                for dst, src in late:
                    sp.dma_start(dst, src).then_inc(late_loaded, 16)
            sp.dma_start(y_base.rearrange("(a n) c -> a (n c)", a=16),
                         x.rearrange("b (h t) c -> (b h) (t c)", h=2)).then_inc(base_copied, 16)
            with sp.Fori(0, PAIRS) as i:
                sp.wait_ge(xn_ready, i + 1)
                sp.dma_start(rows_v[:, bass.ts(i, 2 * Q), 0:C],
                             htok[:, bass.ts(i, 2), :].rearrange("p b (q c) -> p (b q) c", q=Q)).then_inc(rows_stored, 16)
            sp.wait_ge(prob_ready, 1)
            sp.dma_start(rows_v[:, :, C:ROW], prob[:, :, :]).then_inc(probs_stored, 16)
            sp.wait_ge(yo_added, E)
            for s in range(2):
                sp.dma_start(tiles(xtok, s), base_v[s, :, :, :]).then_inc(base_loaded[s], 16)
            with sp.Fori(1, PAIRS) as i:
                for s in range(2):
                    sp.wait_ge(base_loaded[s], i * 16)
                    sp.dma_start(tiles(xtok, i * 2 + s), base_v[i * 2 + s, :, :, :]).then_inc(base_loaded[s], 16)
            with sp.Fori(0, B) as b:
                sp.wait_ge(res_ready, b + 1)
                sp.dma_start(out_v[b, :, :, :], tiles(xtok, b)).then_inc(out_stored, 16)
            sp.wait_ge(out_stored, 16 * B)
            sp.wait_ge(rows_stored, 16 * PAIRS)
            sp.wait_ge(probs_stored, 16)

        @block.gpsimd
        def _(pool):
            n = [0]

            def link(ins):
                n[0] += 1
                ins.then_inc(pool_step, 1)
                pool.wait_ge(pool_step, n[0])

            g = nc.gpsimd
            g.memset(st[:, :, 0:1], NEG_INF)
            g.memset(weps[:, :], WKV_EPS)
            g.memset(wrow[:, :], 1.0)
            g.memset(onesw[:, :], 1.0)
            g.memset(same[:, :], 1.0)
            link(g.memset(ident[:, :], 0.0))
            by_e = same[:, :].rearrange("k (e c) -> k e c", e=E)
            link(g.affine_select(out=by_e, in_=by_e, compare_op=ALU.is_ge, fill=0.0, base=0,
                                 pattern=[[-CH, E], [0, CH]], channel_multiplier=1))
            link(g.affine_select(out=by_e, in_=by_e, compare_op=ALU.is_ge, fill=0.0, base=CH - 1,
                                 pattern=[[CH, E], [0, CH]], channel_multiplier=-1))
            g.affine_select(out=earlier[:, :], in_=same[:, :], compare_op=ALU.is_gt, fill=0.0, base=0,
                            pattern=[[1, P]], channel_multiplier=-1)
            g.iota(centred[:, :].rearrange("p (l e c) -> p l e c", l=2, e=E), pattern=[[P, 2], [0, E], [2 * P, CH]],
                   base=-(NTOK // 2), channel_multiplier=1, allow_small_or_imprecise_dtypes=True)
            g.affine_select(out=ident[:, :], in_=ident[:, :], compare_op=ALU.not_equal, fill=1.0, base=0,
                            pattern=[[-1, P]], channel_multiplier=1).then_inc(consts_ready, 1)

            for k, mine in enumerate(parts):
                pool.wait_ge(mv_ready, k + 1)
                part = slice(mine[0] * Q, (mine[-1] + 1) * Q)
                g.tensor_scalar(va[:, 0, part], mv[:, part, 1], 1.0, LN_EPS, ALU.mult, ALU.add)
                link(g.tensor_scalar(va[:, 1, part], mv[:, part, 1], 1.0 + LN_EPS, LN_EPS * LN_EPS, ALU.mult, ALU.add))
                rsqrt(g, link, 2, part)
                link(g.tensor_tensor(nb[:, part], mv[:, part, 0], rs[:, 1, part], ALU.mult))
                g.tensor_scalar(nb[:, part], nb[:, part], -1.0, 0.0, ALU.mult, ALU.add).then_inc(rs_ready, 1)

            pool.wait_ge(w_loaded, N_LOADS)
            g.tensor_scalar(om[:, :], par[:, :], -1.0, 1.0, ALU.mult, ALU.add)
            g.tensor_scalar(negw[:, :], col["time_decay"], -1.0, 0.0, ALU.mult, ALU.add)
            g.tensor_scalar(wrow[:, :], wrow[:, :], col["time_decay"], None, ALU.mult)
            g.tensor_tensor(wtm[:, :], wtm[:, :], mixrow[:, 0:3, :].rearrange("p n c -> p (n c)"), ALU.mult)
            link(g.tensor_tensor(wcm[:, :].rearrange("p (j c) -> p j c", j=NJ), wcm[:, :].rearrange("p (j c) -> p j c", j=NJ),
                                 mixrow[:, 3:4, :].broadcast_to([P, NJ, C]), ALU.mult))
            pool.sem_inc(weights_ready, 1)

            pool.wait_ge(xp_ready, 1)
            pool.wait_ge(rows_stored, 16 * PAIRS)
            for b in range(B):
                link(g.tensor_scalar(htok[:, b, :], xT[:, b, 0:T], omc["tmr"], None, ALU.mult))
                pool.wait_ge(r_copied, b + 1)
                g.tensor_tensor(rb[:, b, :], rb[:, b, :], htok[:, b, :], ALU.add).then_inc(r_ready, 1)

            pool.wait_ge(probs_stored, 16)
            pool.wait_ge(base_copied, 16)
            pool.wait_ge(idx_ready, 1)

            def gather(e):
                for k in range(NG):
                    g.indirect_dma_start(out=gath[:, e, k, :], out_offset=None, in_=xn_rows[:, :],
                                         in_offset=bass.IndirectOffsetOnAxis(ap=idx[:, e * NG + k:e * NG + k + 1], axis=0),
                                         ).then_inc(gathered[e], 16)

            def scatter(e):
                s = e % 2
                pool.wait_ge(yo_ready, e + 1)
                for k in range(NG):
                    g.indirect_dma_start(out=y_base[:, :],
                                         out_offset=bass.IndirectOffsetOnAxis(ap=idx[:, e * NG + k:e * NG + k + 1], axis=0),
                                         in_=yo[:, s, k, :], in_offset=None, compute_op=ALU.add).then_inc(scattered[s], 16)

            def landed(e):
                pool.wait_ge(scattered[e % 2], 16 * NG * (e // 2 + 1))
                pool.sem_inc(yo_added, 1)

            ahead = 4
            gather(0)
            link(g.memset(mid[:, :, len(FJ) - 1, :], 1.0))
            pool.sem_inc(mid_ones, 1)
            for e in range(1, ahead):
                gather(e)
            for e in range(E):
                if e:
                    landed(e - 1)
                scatter(e)
                if e + ahead < E:
                    gather(e + ahead)
            landed(E - 1)

        @block.scalar
        def _(act):
            a = nc.scalar
            for dst, src in loads:
                act.dma_start(dst, src).then_inc(w_loaded, 16)
            a.preload_act_table_set("natural_log_exp_and_others")
            for b in range(B):
                act.wait_ge(xT_psum, b + 1)
                a.copy(xT[:, b, 1:T + 1], tp[b % 2][:, :]).then_inc(xT_ready, 1)
                act.wait_ge(rs_ready, rs_part[b])
                act.wait_ge(x_loaded[b], 16)
                for q in range(Q):
                    f = b * Q + q
                    last = a.activation(vb[:, b, P * q:P * q + P], xtok[:, b, P * q:P * q + P], ACT.Identity,
                                        bias=nb[:, f:f + 1], scale=rs[:, 1, f:f + 1])
                last.then_inc(h_ready, 1)
            act.wait_ge(lmax_ready, 1)
            a.activation(prob[:, :, :], prob[:, :, :], ACT.Exp).then_inc(lexp_ready, 1)
            act.wait_ge(w_loaded, N_LOADS)

            def h_channel_major(b):
                act.wait_ge(hT_psum, b + 1)
                a.activation(ca[:, b, :], tp[b == 1][:, :], ACT.Identity, bias=col["b1"], scale=col["g1"]).then_inc(hT_ready, 1)

            def copy_r(b):
                act.wait_ge(r_psum, b + 1)
                a.copy(rb[:, b, :], kvr_ps[b % 2][2][:, :]).then_inc(r_copied, 1)

            def abexp(i):
                act.wait_ge(ab_ready, i + 1)
                act.wait_ge(r_psum, 2 * i + 2)
                a.activation(ca[:, 2 * i:2 * i + 2, :], kd[:, 2 * i:2 * i + 2, :], ACT.Relu, bias=negw[:, 0:1]).then_inc(relu_ready, 1)
                act.wait_ge(relu_ready, i + 1)
                a.activation(ca[:, 2 * i:2 * i + 2, :], ca[:, 2 * i:2 * i + 2, :], ACT.Exp, scale=-1.0)
                a.activation(cb[:, 2 * i:2 * i + 2, :], cb[:, 2 * i:2 * i + 2, :], ACT.Exp).then_inc(abexp_ready, 1)

            for i in range(PAIRS):
                if i == 0:
                    h_channel_major(0)
                    h_channel_major(1)
                copy_r(2 * i)
                if i < PAIRS - 1:
                    h_channel_major(2 * i + 2)
                copy_r(2 * i + 1)
                if i < PAIRS - 1:
                    h_channel_major(2 * i + 3)
                abexp(i)

            def ln(i):
                act.wait_ge(s_ready, 2 * i + 2)
                a.activation(st[:, 2 * i:2 * i + 2, 0:T], st[:, 2 * i:2 * i + 2, 0:T], ACT.Ln,
                             bias=weps[:, 0:1]).then_inc(lns_ready, 1)

            def eexp(i):
                act.wait_ge(e_ready, i + 1)
                a.activation(ca[:, 2 * i:2 * i + 2, :], ca[:, 2 * i:2 * i + 2, :], ACT.Exp, scale=-1.0)
                a.activation(cb[:, 2 * i:2 * i + 2, :], cb[:, 2 * i:2 * i + 2, :], ACT.Exp).then_inc(eexp_ready, 1)

            def gates(i):
                act.wait_ge(e_ready, i + 1)
                if i == 0:
                    act.wait_ge(r_ready, B)
                a.activation(kd[:, 2 * i:2 * i + 2, :], kd[:, 2 * i:2 * i + 2, :], ACT.Sigmoid, bias=col["time_first"])
                a.activation(rb[:, 2 * i:2 * i + 2, :], rb[:, 2 * i:2 * i + 2, :], ACT.Sigmoid).then_inc(gates_ready, 1)

            def expert(e):
                s = e % 2
                act.wait_ge(gT_psum, e + 1)
                a.copy(xg[:, s, :], moe[s][:, :]).then_inc(xg_ready, 1)
                if e == 0:
                    act.wait_ge(mid_ones, 1)
                    act.wait_ge(late_loaded, N_LATE)
                for j, fj in enumerate(FJ):
                    act.wait_ge(up_psum, e * len(FJ) + (j + 1))
                    a.activation(mid[0:fj, s, j, :], moe[(s + 1 + j) % 2][0:fj, :], ACT.Silu,
                                 bias=bup[0:fj, e // EG, j:j + 1]).then_inc(mid_ready, 1)
                act.wait_ge(down_psum, e + 1)
                if e >= 2:
                    act.wait_ge(yo_added, e - 1)
                for k in range(NG):
                    last = a.activation(yo[:, s, k, :], moe[s][:, C * k:C * k + C], ACT.Copy,
                                        scale=gath[:, e, k, C + e:C + e + 1])
                last.then_inc(yo_ready, 1)

            def x1tok(i):
                for b in (2 * i, 2 * i + 1):
                    n = tp_turn["x1tok", b]
                    act.wait_ge(tp_filled, n + 1)
                    a.copy(ca[:, b, :], tp[n % 2][:, :]).then_inc(tp_copied, 1)

            def xn2T(i):
                for b in (2 * i, 2 * i + 1):
                    n = tp_turn["xn2T", b]
                    act.wait_ge(tp_filled, n + 1)
                    a.activation(rb[:, b, :], tp[n % 2][:, :], ACT.Identity, bias=col["b2"], scale=col["g2"])\
                        .then_inc(tp_copied, 1)

            def rr(i):
                act.wait_ge(z_ready, i + 1)
                a.activation(cb[:, 2 * i:2 * i + 2, :], cb[:, 2 * i:2 * i + 2, :], ACT.Sigmoid).then_inc(rr_ready, 1)

            def squares(b):
                s = b % 2
                for j in range(NJ):
                    act.wait_ge(kk_ready, b * NJ + (j + 1))
                    a.activation(rel[:, s, j, :], rel[:, s, j, :], ACT.Relu).then_inc(act_step, 1)
                    act.wait_ge(act_step, b * NJ + (j + 1))
                    a.activation(rel[:, s, j, :], rel[:, s, j, :], ACT.Square).then_inc(sq_ready, 1)

            def x2tok(b):
                n = tp_turn["x2tok", b]
                act.wait_ge(tp_filled, n + 1)
                a.copy(ca[:, b, :], tp[n % 2][:, :]).then_inc(tp_copied, 1)

            for kind, n in ORDER:
                {"ln": ln, "eexp": eexp, "gates": gates, "expert": expert, "x1tok": x1tok, "xn2T": xn2T, "rr": rr,
                 "squares": squares, "x2tok": x2tok}.get(kind, lambda n: None)(n)

        @block.vector
        def _(dve):
            v = nc.vector
            steps = [0]
            per = [0, 0]

            def link(ins):
                per[0] += 1
                ins.then_inc(dve_step, 1)
                dve.wait_ge(dve_step, per[1] + (steps[0] + per[0]))

            def turn(i, size):
                steps[0] += per[0] if not isinstance(per[1], int) or per[1] == 0 else 0
                per[0], per[1] = 0, i * size

            def turned(size, turns):
                assert per[0] == size, (per[0], size)
                steps[0] += size * turns
                per[0], per[1] = 0, 0

            def statistics(t, b):
                for q in range(Q):
                    last = v.bn_stats(stats[:, b * Q + q, :], t[:, b, P * q:P * q + P])
                return last

            def aggregate(b):
                for q in range(Q):
                    last = v.bn_aggr(mv[:, b * Q + q, :], stats[:, b * Q + q, :])
                return last

            def normalise(dst, src, b, k):
                for q in range(Q):
                    f = b * Q + q
                    last = v.tensor_scalar(dst[:, b, P * q:P * q + P], src[:, b, P * q:P * q + P], mv[:, f, 0:1],
                                           rs[:, k, f:f + 1], ALU.subtract, ALU.mult)
                return last

            for n in range(len(parts) + 1):
                if n < len(parts):
                    for b in parts[n]:
                        dve.wait_ge(x_loaded[b], 16)
                        last = statistics(xtok, b)
                    link(last)
                    for b in parts[n]:
                        last = aggregate(b)
                    last.then_inc(mv_ready, 1)
                if n >= 1:
                    dve.wait_ge(rs_ready, n)
                    for b in parts[n - 1]:
                        last = normalise(htok, xtok, b, 0)
                    last.then_inc(xn_ready, 1)

            def mix(dst, b, name, psum, psum_sem, ready, first=0):
                dve.wait_ge(psum_sem, b + (1 + first))
                v.scalar_tensor_tensor(dst[:, b, :], xT[:, b, 0:T], omc[name], psum[:, :],
                                       ALU.mult, ALU.add).then_inc(ready, 1)

            def coefficients(i, ready):
                d = kd[:, bass.ts(i, 2), :]
                if ready is e_ready:
                    v.tensor_scalar(ca[:, bass.ts(i, 2), :], d, col["time_decay"], 0.0, ALU.subtract, ALU.max)
                v.tensor_scalar(cb[:, bass.ts(i, 2), :], d, col["time_decay"], 0.0, ALU.subtract, ALU.min)\
                    .then_inc(ready, 1)

            dve.wait_ge(logits_psum, B)
            dve.wait_ge(w_loaded, N_LOADS)
            link(v.tensor_tensor(prob[:, :, :], lg, brr[:, :].unsqueeze(1).broadcast_to([P, NF, E]), ALU.add))
            link(v.tensor_reduce(rmax[:, :], prob[:, :, :], AX.X, ALU.max))
            v.tensor_tensor(prob[:, :, :], prob[:, :, :], rmax[:, :].unsqueeze(2).broadcast_to([P, NF, E]), ALU.subtract)\
                .then_inc(lmax_ready, 1)
            dve.wait_ge(xT_ready, B)
            v.tensor_copy(xT[:, :, 0:1], xT[:, :, 1:2]).then_inc(xp_ready, 1)
            dve.wait_ge(lexp_ready, 1)
            link(v.tensor_reduce(rmax[:, :], prob[:, :, :], AX.X, ALU.add))
            link(v.reciprocal(rmax[:, :], rmax[:, :]))
            v.tensor_tensor(prob[:, :, :], prob[:, :, :], rmax[:, :].unsqueeze(2).broadcast_to([P, NF, E]), ALU.mult)\
                .then_inc(prob_ready, 1)
            dve.wait_ge(prob_ready, 1)
            for h in range(2):
                last = v.tensor_scalar(pcl[:, h, :, :].rearrange("p e c -> p c e"), prob[:, h:NF:2, :], TINY, SCALE, ALU.max, ALU.mult)
            last.then_inc(pcl_ready, 1)

            def reach():
                with nc.allow_low_precision(reason="counts up to 256 are exact in bfloat16"):
                    v.tensor_scalar(hit[:, :], pE[:, :], cand[:, 0:1], 0.0, ALU.is_ge, ALU.add, accum_out=cnt[:, 0:1])\
                        .then_inc(cnt_ready, 1)

            def exponent_step(n):
                dve.wait_ge(count_psum, n + 1)
                h = EXP_STEPS[n] / 2
                if h >= 1:
                    link(v.tensor_scalar(ok[:, :], cps, KTOP - 0.5, 2.0 ** h - 2.0 ** -h, ALU.is_ge, ALU.mult))
                    link(v.scalar_tensor_tensor(cand[:, :], ok[:, :], 2.0 ** -h, cand[:, :], ALU.add, ALU.mult))
                    reach()

            def mantissa_step(n):
                dve.wait_ge(count_psum, n + len(EXP_STEPS) + 1)
                link(v.tensor_scalar(ok[:, :], cps, KTOP - 0.5, 0.5, ALU.is_ge, ALU.subtract))
                link(v.scalar_tensor_tensor(cand[:, :], ok[:, :], delta[:, 0:1], cand[:, :], ALU.mult, ALU.add))
                reach()
                v.tensor_scalar(delta[:, :], delta[:, :], 0.5, None, ALU.mult)

            def running_max(b):
                dve.wait_ge(k_ready, b + 1)
                v.tensor_tensor_scan(st[:, b, 1:T + 1], wrow[:, :], kd[:, b, :], NEG_INF,
                                     ALU.add, ALU.max).then_inc(m_ready, 1)

            def below_max(i):
                dve.wait_ge(m_ready, i * 2 + 2)
                link(v.tensor_tensor(kd[:, bass.ts(i, 2), :], kd[:, bass.ts(i, 2), :], st[:, bass.ts(i, 2), 0:T], ALU.subtract))

            def mix_k(b, s):
                mix(kd, b, "tmk", kvr_ps[s][0], k_psum, k_ready)

            def mix_v(b, s):
                mix(vb, b, "tmv", kvr_ps[s][1], v_psum, v_ready)

            dve.wait_ge(xp_ready, 1)
            v.memset(cand[:, :], TINY * SCALE * 2.0 ** EXP_STEPS[0])
            dve.wait_ge(weights_ready, 1)
            dve.wait_ge(pE_psum, 1)
            link(v.tensor_copy(pE[:, :], pt_ps))
            dve.sem_inc(pE_ready, 1)
            reach()
            for b in range(2):
                mix_k(b, b)
                exponent_step(3 * b)
                mix_v(b, b)
                exponent_step(3 * b + 1)
                running_max(b)
                exponent_step(3 * b + 2)
            below_max(0)
            exponent_step(6)
            link(v.tensor_scalar(ok[:, :], cps, KTOP - 0.5, 0.5, ALU.is_ge, ALU.mult))
            link(v.scalar_tensor_tensor(cand[:, :], ok[:, :], 0.5, cand[:, :], ALU.add, ALU.mult))
            link(v.tensor_scalar(delta[:, :], cand[:, :], 0.5, None, ALU.mult))
            link(v.tensor_scalar(cand[:, :], cand[:, :], 1.5, None, ALU.mult))
            reach()
            coefficients(0, ab_ready)
            mantissa_step(0)

            with dve.Fori(1, PAIRS) as i:
                turn(i - 1, 2 * TURN_STEPS + 1)
                for s in range(2):
                    b = i * 2 + s
                    mix_k(b, s)
                    mantissa_step(i * TURN_STEPS + (3 * s + 1 - TURN_STEPS))
                    mix_v(b, s)
                    mantissa_step(i * TURN_STEPS + (3 * s + 2 - TURN_STEPS))
                    running_max(b)
                    mantissa_step(i * TURN_STEPS + (3 * s + 3 - TURN_STEPS))
                below_max(i)
                mantissa_step(i * TURN_STEPS)
                coefficients(i, ab_ready)
            turned(2 * TURN_STEPS + 1, PAIRS - 1)
            dve.wait_ge(count_psum, len(EXP_STEPS) + MAN_BITS)
            link(v.tensor_scalar(ok[:, :], cps, KTOP - 0.5, 1.0, ALU.is_ge, ALU.subtract))
            link(v.scalar_tensor_tensor(cand[:, :], ok[:, :], delta[:, 0:1], cand[:, :], ALU.mult, ALU.add))

            def exp_sum(b):
                dve.wait_ge(abexp_ready, b // 2 + 1)
                v.tensor_tensor_scan(st[:, b, 1:T + 1], ca[:, b, :], cb[:, b, :], 1.0, ALU.mult, ALU.add)\
                    .then_inc(s_ready, 1)

            with nc.allow_low_precision(reason="counts up to 256 are exact in bfloat16"):
                v.tensor_scalar(gt[:, :], pE[:, :], cand[:, 0:1], 0.0, ALU.is_gt, ALU.add, accum_out=gtc[:, 0:1])
                v.tensor_scalar(eq[:, :], pE[:, :], cand[:, 0:1], 0.0, ALU.is_equal, ALU.add, accum_out=eqc[:, 0:1])\
                    .then_inc(ties_ready, 1)
            link(v.memset(st[:, :, 0:1], 1.0))
            dve.wait_ge(ties_ready, 1)
            link(v.tensor_tensor_scan(rank[:, :], onesw[:, :], eq[:, :], 0.0, ALU.mult, ALU.add))
            dve.wait_ge(ties_psum, 1)
            link(v.tensor_scalar(need[:, :], sel_ps[:, 0:1], -1.0, float(KTOP), ALU.mult, ALU.add))
            link(v.tensor_tensor(need[:, :], need[:, :], sel_ps[:, 1:2], ALU.subtract))
            link(v.scalar_tensor_tensor(eq[:, :], rank[:, :], need[:, 0:1], eq[:, :], ALU.is_le, ALU.mult))
            link(v.tensor_tensor(gt[:, :], gt[:, :], eq[:, :], ALU.add))
            link(v.tensor_tensor_scan(rank[:, :], onesw[:, :], gt[:, :], 0.0, ALU.mult, ALU.add))
            v.tensor_copy(selc[:, :], rank[:, W - 1:W]).then_inc(selc_ready, 1)
            exp_sum(0)
            dve.wait_ge(selc_psum, 1)
            link(v.tensor_copy(need[:, :], sel_ps[:, 2:3]))
            v.scalar_tensor_tensor(eq[:, :], rank[:, :], need[:, 0:1], gt[:, :], ALU.add, ALU.mult).then_inc(slot_ready, 1)
            exp_sum(1)
            dve.wait_ge(slot_psum, 1)
            link(v.tensor_scalar(slot[:, :], sl_ps[:, 0:2 * P], -1.0, None, ALU.add))
            v.tensor_scalar(slot_hi[:, :], slot[:, :], 5, None, ALU.arith_shift_right)
            link(v.tensor_scalar(slot_lo[:, :], slot[:, :], LO - 1, None, ALU.bitwise_and))
            v.tensor_copy(hi16[:, :], slot_hi[:, :])
            link(v.tensor_copy(lo16[:, :], slot_lo[:, :]))
            dve.wait_ge(rows_stored, 16 * PAIRS)
            dve.wait_ge(h_ready, B)
            dve.wait_ge(r_ready, B)
            for h in range(HI):
                last = v.tensor_scalar(oh_hi[:, h, :], hi16[:, :], float(h), None, ALU.is_equal)
            link(last)
            v.tensor_tensor(oh_hi[:, :, :], oh_hi[:, :, :], centred[:, :].unsqueeze(1).broadcast_to([P, HI, 2 * P]), ALU.mult)
            for l in range(LO):
                last = v.tensor_scalar(oh_lo[:, l, :], lo16[:, :], float(l), None, ALU.is_equal)
            last.then_inc(onehot_ready, 1)
            for b in range(2, B):
                exp_sum(b)

            def above_state(i):
                dve.wait_ge(lns_ready, i + 1)
                link(v.tensor_tensor(kd[:, bass.ts(i, 2), :], kd[:, bass.ts(i, 2), :], st[:, bass.ts(i, 2), 0:T], ALU.subtract))
                coefficients(i, e_ready)

            above_state(0)
            dve.wait_ge(idx_psum, 1)
            f_v = idxf[:, :].rearrange("l (e h) -> l e h", e=E)
            link(v.tensor_scalar(f_v, idx_ps, float(NTOK // 2), None, ALU.add))
            f_g = idxf[:, :].rearrange("l (n j) -> l n j", j=P // LO)
            for j in range(P // LO):
                last = v.tensor_copy(idx[LO * j:LO * j + LO, :], f_g[:, :, j])
            last.then_inc(idx_ready, 1)

            with dve.Fori(1, PAIRS) as i:
                turn(i - 1, 1)
                above_state(i)
            turned(1, PAIRS - 1)

            dve.wait_ge(lns_ready, PAIRS)
            link(v.memset(st[:, :, 0:1], 0.0))
            with dve.Fori(0, PAIRS) as i:
                turn(i, 1)
                dve.wait_ge(eexp_ready, i + 1)
                link(v.tensor_tensor(cb[:, bass.ts(i, 2), :], cb[:, bass.ts(i, 2), :], vb[:, bass.ts(i, 2), :], ALU.mult))
                for s in range(2):
                    b = i * 2 + s
                    v.tensor_tensor_scan(st[:, b, 1:T + 1], ca[:, b, :], cb[:, b, :], 0.0, ALU.mult, ALU.add)\
                        .then_inc(aa_ready, 1)
            turned(1, PAIRS)

            def attended(i):
                pr = slice(2 * i, 2 * i + 2)
                dve.wait_ge(gates_ready, i + 1)
                dve.wait_ge(aa_ready, i * 2 + 2)
                y, aa, x1 = ca[:, pr, :], st[:, pr, 0:T], xT[:, pr, 1:T + 1]
                link(v.tensor_tensor(y, vb[:, pr, :], aa, ALU.subtract))
                link(v.tensor_tensor(y, y, kd[:, pr, :], ALU.mult))
                link(v.tensor_tensor(y, y, aa, ALU.add))
                link(v.tensor_tensor(y, y, rb[:, pr, :], ALU.mult))
                link(v.tensor_tensor(x1, y, x1, ALU.add))
                v.tensor_copy(xT[:, pr, 0:1], xT[:, pr, T:T + 1]).then_inc(x1_ready, 1)

            def normalise_x1(i):
                mine = (2 * i, 2 * i + 1)
                for b in mine:
                    dve.wait_ge(tp_copied, tp_turn["x1tok", b] + 1)
                    last = statistics(ca, b)
                link(last)
                for b in mine:
                    last = aggregate(b)
                link(last)
                part = slice(mine[0] * Q, (mine[-1] + 1) * Q)
                link(v.tensor_scalar(va[:, 0, part], mv[:, part, 1], LN_EPS, None, ALU.add))
                rsqrt(v, link, 1, part)
                for b in mine:
                    normalise(ca, ca, b, 0).then_inc(xn2_ready, 1)

            def mix_terms(i):
                pr = slice(2 * i, 2 * i + 2)
                xp = xT[:, pr, 0:T]
                v.tensor_scalar(kd[:, pr, :], xp, omc["cmk"], None, ALU.mult)
                link(v.tensor_scalar(cb[:, pr, :], xp, omc["cmr"], None, ALU.mult))

            def receptance(i):
                pr = slice(2 * i, 2 * i + 2)
                dve.wait_ge(tp_copied, tp_turn["xn2T", 2 * i + 1] + 1)
                v.scalar_tensor_tensor(cb[:, pr, :], rb[:, pr, :], col["cmr"], cb[:, pr, :], ALU.mult, ALU.add)\
                    .then_inc(z_ready, 1)

            def hidden(b):
                if b >= 2:
                    dve.wait_ge(vv_psum, b - 1)
                for j in range(NJ):
                    n = NJ * b + j
                    dve.wait_ge(kk_psum, n + 1)
                    v.tensor_tensor(rel[:, b % 2, j, :], kk_ps[n % 3][:, :], kd[:, b, :], ALU.add).then_inc(kk_ready, 1)

            def x2(b):
                dve.wait_ge(vv_psum, b + 1)
                dve.wait_ge(rr_ready, b // 2 + 1)
                link(v.tensor_tensor(st[:, b, 0:T], mv_ps[:, :], cb[:, b, :], ALU.mult))
                v.tensor_tensor(st[:, b, 0:T], st[:, b, 0:T], xT[:, b, 1:T + 1], ALU.add).then_inc(x2_ready, 1)

            for stage, n in [(attended, 0), (attended, 1), (mix_terms, 0), (normalise_x1, 0), (attended, 2), (receptance, 0),
                             (mix_terms, 1), (normalise_x1, 1), (hidden, 0), (attended, 3), (receptance, 1), (hidden, 1),
                             (mix_terms, 2), (normalise_x1, 2), (x2, 0), (hidden, 2), (receptance, 2), (x2, 1), (hidden, 3),
                             (mix_terms, 3), (normalise_x1, 3), (x2, 2), (hidden, 4), (receptance, 3), (x2, 3), (hidden, 5),
                             (x2, 4), (hidden, 6), (x2, 5), (hidden, 7), (x2, 6), (x2, 7)]:
                stage(n)

            for b in range(B):
                dve.wait_ge(tp_copied, tp_turn["x2tok", b] + 1)
                dve.wait_ge(base_loaded[b % 2], 16 * (b // 2 + 1))
                v.tensor_tensor(xtok[:, b, :], xtok[:, b, :], ca[:, b, :], ALU.add).then_inc(res_ready, 1)

        @block.tensor
        def _(pe):
            t = nc.tensor

            def wait(s, value):
                if value > 0:
                    pe.wait_ge(s, value)

            pe.wait_ge(consts_ready, 1)

            def logits(b):
                if b == 0:
                    pe.wait_ge(w_loaded, N_LOADS)
                wait(xT_ready, b + 1)
                for q in range(Q):
                    last = t.matmul(lg[:, Q * b + q, :], xT[:, b, 1 + P * q:1 + P * q + P], wr[:, :], start=True, stop=True)
                last.then_inc(logits_psum, 1)

            for b in range(B):
                wait(xn_ready, b // 2 + 1)
                wait(xT_ready, b - 1)
                for q in range(Q):
                    last = t.transpose(tp[b % 2][:, P * q:P * q + P], htok[:, b, P * q:P * q + P], ident[:, :])
                last.then_inc(xT_psum, 1)
                if b:
                    logits(b - 1)
            logits(B - 1)

            def h_transposed(b):
                wait(h_ready, b + 1)
                wait(hT_ready, 1 if b == 2 else b if b > 2 else 0)
                for q in range(Q):
                    last = t.transpose(tp[b == 1][:, P * q:P * q + P], vb[:, b, P * q:P * q + P], ident[:, :])
                last.then_inc(hT_psum, 1)

            def kvr(b, n):
                ready, done = ((k_ready, k_psum), (v_ready, v_psum), (r_copied, r_psum))[n]
                wait(hT_ready, b + 1)
                wait(ready, b - 1)
                t.matmul(kvr_ps[b % 2][n][:, :], wtm[:, C * n:C * n + C], ca[:, b, :], start=True, stop=True).then_inc(done, 1)

            h_transposed(0)
            h_transposed(1)
            pe.wait_ge(weights_ready, 1)
            kvr(0, 0)
            pe.wait_ge(pcl_ready, 1)
            for h in range(2):
                last = t.transpose(pt_ps[:, P * h:P * h + P], pcl[:, h, :, :].rearrange("p e c -> p (e c)"), ident[:, :])
            last.then_inc(pE_psum, 1)
            kvr(0, 1)
            kvr(0, 2)
            for n in range(-1, len(EXP_STEPS) + MAN_BITS):
                if n == 0:
                    pe.wait_ge(pE_ready, 1)
                if n >= 0:
                    pe.wait_ge(cnt_ready, n + 1)
                    t.matmul(cps, same[:, :], cnt[:, :], start=True, stop=True).then_inc(count_psum, 1)
                for b in range(1, B):
                    if b >= 2 and n == position(b) - 5:
                        h_transposed(b)
                    if n in range(position(b) - 4, position(b) - 1):
                        kvr(b, n - (position(b) - 4))

            pe.wait_ge(ties_ready, 1)
            t.matmul(sel_ps[:, 0:1], same[:, :], gtc[:, :], start=True, stop=True)
            t.matmul(sel_ps[:, 1:2], earlier[:, :], eqc[:, :], start=True, stop=True).then_inc(ties_psum, 1)
            pe.wait_ge(selc_ready, 1)
            t.matmul(sel_ps[:, 2:3], earlier[:, :], selc[:, :], start=True, stop=True).then_inc(selc_psum, 1)
            pe.wait_ge(slot_ready, 1)
            pe.wait_ge(r_copied, B)
            for h in range(2):
                last = t.transpose(sl_ps[:, P * h:P * h + P], eq[:, P * h:P * h + P], ident[:, :])
            last.then_inc(slot_psum, 1)

            pe.wait_ge(onehot_ready, 1)
            for e in range(E):
                for f in range(NF):
                    n = (f % 2) * P + e * CH + f // 2
                    last = t.matmul(idx_ps[:, e, :], oh_lo[:, :, n], oh_hi[:, :, n],
                                    start=(f == 0), stop=(f == NF - 1))
            last.then_inc(idx_psum, 1)

            def expert(e):
                s = e % 2
                if e == 0:
                    pe.wait_ge(late_loaded, N_LATE)
                pe.wait_ge(gathered[e], 16 * NG)
                wait(mid_ready, len(FJ) * e)
                wait(yo_ready, e - 1)
                for k in range(NG):
                    last = t.transpose(moe[s][:, P * k:P * k + P], gath[:, e, k, 0:C], ident[:, :])
                last.then_inc(gT_psum, 1)
                wait(yo_ready, e)
                wait(xg_ready, e + 1)
                for j, fj in enumerate(FJ):
                    if j == 2:
                        wait(mid_ready, len(FJ) * e + 1)
                    t.matmul(moe[(s + 1 + j) % 2][0:fj, :], wup[:, e // EG, P * j:P * j + fj], xg[:, s, :],
                             start=True, stop=True).then_inc(up_psum, 1)
                wait(mid_ready, len(FJ) * (e + 1))
                for k in range(NG):
                    for j, fj in enumerate(FJ):
                        rows = fj + (j == len(FJ) - 1)
                        last = t.matmul(moe[s][:, C * k:C * k + C], mid[0:rows, s, j, P * k:P * k + P],
                                        wdn[0:rows, e, j, :], start=(j == 0), stop=(j == len(FJ) - 1))
                last.then_inc(down_psum, 1)

            def transposed(kind, b, src):
                n = tp_turn[kind, b]
                wait(tp_copied, n - 1)
                for q in range(Q):
                    last = t.transpose(tp[n % 2][:, P * q:P * q + P], src[:, P * q:P * q + P], ident[:, :])
                last.then_inc(tp_filled, 1)

            def x1tok(i):
                pe.wait_ge(x1_ready, i + 1)
                if i == 0:
                    pe.wait_ge(idx_ready, 1)
                for b in (2 * i, 2 * i + 1):
                    transposed("x1tok", b, xT[:, b, 1:T + 1])

            def xn2T(i):
                for b in (2 * i, 2 * i + 1):
                    pe.wait_ge(xn2_ready, b + 1)
                    transposed("xn2T", b, ca[:, b, :])

            def up(b):
                wait(tp_copied, tp_turn["xn2T", b] + 1)
                for j in range(NJ):
                    n = NJ * b + j
                    wait(kk_ready, n - 2)
                    t.matmul(kk_ps[n % 3][:, :], wcm[:, C * j:C * j + C], rb[:, b, :], start=True, stop=True).then_inc(kk_psum, 1)

            def down(b):
                wait(x2_ready, b)
                for j in range(NJ):
                    wait(sq_ready, NJ * b + j + 1)
                    last = t.matmul(mv_ps[:, :], wcp[:, j, :], rel[:, b % 2, j, :], start=(j == 0), stop=(j == NJ - 1))
                last.then_inc(vv_psum, 1)

            def x2tok(b):
                pe.wait_ge(x2_ready, b + 1)
                transposed("x2tok", b, st[:, b, 0:T])

            for kind, n in ORDER:
                {"expert": expert, "x1tok": x1tok, "xn2T": xn2T, "up": up, "down": down, "x2tok": x2tok}\
                    .get(kind, lambda n: None)(n)


def kernel(**inputs):
    import numpy as _np
    import concourse.bacc as _bacc
    from concourse import mybir as _mybir
    from concourse.bass_utils import run_bass_kernel_spmd as _run

    nc = _bacc.Bacc("TRN2", target_bir_lowering=False, num_devices=1)
    given = {n[len("L0_"):]: _np.asarray(a) for n, a in inputs.items()}
    chan = {n: given["attn_" + n].reshape(-1) for n in PARAMS}
    laid_out = {
        "x": given["attn_x"],
        "chan_cols": _np.stack([chan[n] for n in PARAMS], axis=1),
        "chan_rows": _np.stack([chan[n] for n in MIXES]),
        "W_tm": given["attn_W_tm"], "W_cm": given["attn_W_cm"], "W_cp": given["attn_W_cp"],
        "Wr": given["ffn_Wr"], "br": given["ffn_br"], "W_up": given["ffn_W_up"], "b_up_t": given["ffn_b_up"].T,
        "W_down": given["ffn_W_down"], "b_down": given["ffn_b_down"],
    }
    arrays, args = {}, []
    for name, a in laid_out.items():
        a = _np.ascontiguousarray(a)
        arrays[f"in_{name}"] = a
        args.append(nc.dram_tensor(f"in_{name}", a.shape, _mybir.dt.from_np(a.dtype), kind="ExternalInput").ap())
    shape = laid_out["x"].shape
    args.append(nc.dram_tensor("out_0", shape, _mybir.dt.float32, kind="ExternalOutput").ap())
    rwkv_plus_expert_choice(nc, *args)
    r = _run(nc, [arrays], core_ids=[0])
    return r.results[0]["out_0"]
```

```python
from contextlib import ExitStack

import concourse.bass as bass
from concourse import mybir

ALU = mybir.AluOpType
ACT = mybir.ActivationFunctionType
F32 = mybir.dt.float32
F16 = mybir.dt.float16
BF16 = mybir.dt.bfloat16
I32 = mybir.dt.int32
U32 = mybir.dt.uint32
AX = mybir.AxisListType

PARAMS = ["time_decay", "time_first", "g1", "b1", "tmk", "tmv", "tmr", "g2", "b2", "cmk", "cmr"]
MIXES = ["tmk", "tmv", "tmr", "cmk"]


def rwkv_plus_expert_choice(nc, x, chan_cols, chan_rows, W_tm, W_cm, W_cp, Wr, br, W_up, b_up_t, W_down, b_down, out):
    B, T, C = x.shape
    E = Wr.shape[1]
    NGRP, _, F = W_up.shape
    EG = E // NGRP
    P = 128
    assert C == P and T == 4 * P and E == B and EG == 2
    Q = T // P
    NTOK = B * T
    NF = B * Q
    KTOP = NTOK // E
    NG = KTOP // P
    FJ = [min(P, F - P * j) for j in range((F + P - 1) // P)]
    NJ = W_cm.shape[1] // C
    TP = T + 2
    ROW = C + E
    PAIRS = B // 2
    LN_EPS, WKV_EPS, NEG_INF = 1e-5, 1e-8, -1e38
    LO, HI = 32, KTOP // 32

    TINY, SCALE = 2.0 ** -126, 2.0 ** 100
    EXP_STEPS = (64, 32, 16, 8, 4, 2, 1)
    MAN_BITS = 23
    TURN_STEPS = 7
    assert len(EXP_STEPS) == 7 and 1 + TURN_STEPS * (PAIRS - 1) + 1 == MAN_BITS
    CH = P // E
    W = NTOK // CH

    xn_rows = nc.dram_tensor("xn_rows", [NTOK, ROW], F32, kind="Internal").ap()
    x_v = x.rearrange("b (q p) c -> b p q c", q=Q)
    out_v = out.rearrange("b (q p) c -> b p q c", q=Q)
    out_rows = out.rearrange("b t c -> (b t) c")
    rows_v = xn_rows.rearrange("(f p) c -> p f c", p=P)

    ctx = ExitStack()
    with ctx:
        def sb(name, shape, dt=F32):
            return ctx.enter_context(nc.sbuf_tensor(name, shape, dt))

        def pb(name, shape, dt=F32):
            return ctx.enter_context(nc.psum_tensor(name, shape, dt))

        def sem(name):
            return ctx.enter_context(nc.semaphore(name))

        xtok = sb("xtok", [P, B, T])
        htok = sb("htok", [P, B, T])
        xT = sb("xT", [P, B, TP])
        kd = sb("kd", [P, B, T])
        st = sb("st", [P, B, TP])
        vb = sb("vb", [P, B, T])
        rb = sb("rb", [P, B, T])
        ca = sb("ca", [P, B, T])
        cb = sb("cb", [P, B, T])
        rel = vb[:, :, :].rearrange("p (s j) t -> p s j t", s=2)

        par = sb("par", [P, len(PARAMS)])
        om = sb("om", [P, len(PARAMS)])
        negw = sb("negw", [P, 1])
        col = {n: par[:, i:i + 1] for i, n in enumerate(PARAMS)}
        omc = {n: om[:, i:i + 1] for i, n in enumerate(PARAMS)}
        wrow = sb("wrow", [P, T])
        mixrow = sb("mixrow", [P, len(MIXES), C])
        wtm = sb("wtm", [P, 3 * C])
        wcm = sb("wcm", [P, NJ * C])
        wcp = sb("wcp", [P, NJ, C])
        wr = sb("wr", [P, E])
        brc = sb("brc", [E, 1])
        wup = sb("wup", [P, NGRP, F])
        bup = sb("bup", [P, NGRP, len(FJ)])
        wdn = sb("wdn", [P, E, len(FJ), C])
        ident = sb("ident", [P, P])
        same = sb("same", [P, P], BF16)
        earlier = sb("earlier", [P, P], BF16)
        weps = sb("weps", [P, 1])

        stats = sb("stats", [P, NF, 6])
        mv = sb("mv", [P, NF, 2])
        rs = sb("rs", [P, 2, NF])
        nt = sb("nt", [P, 2, NF])
        va = sb("va", [P, 2, NF])
        nb = sb("nb", [P, NF])

        prob = sb("prob", [P, NF, E])
        pcl = sb("pcl", [P, 2, E, CH])
        rmax = sb("rmax", [P, NF])
        pE = sb("pE", [P, W])
        hit = sb("hit", [P, W], BF16)
        cand = sb("cand", [P, 1])
        delta = sb("delta", [P, 1])
        ok = sb("ok", [P, 1])
        cnt = sb("cnt", [P, 1], BF16)
        gtc = sb("gtc", [P, 1], BF16)
        eqc = sb("eqc", [P, 1], BF16)
        selc = sb("selc", [P, 1], BF16)
        need = sb("need", [P, 1])
        gt = sb("gt", [P, W])
        eq = sb("eq", [P, W])
        rank = sb("rank", [P, W])
        onesw = sb("onesw", [P, W])
        slot = sb("slot", [P, 2 * P], I32)
        slot_hi = sb("slot_hi", [P, 2 * P], I32)
        slot_lo = sb("slot_lo", [P, 2 * P], I32)
        hi16 = sb("hi16", [P, 2 * P], F16)
        lo16 = sb("lo16", [P, 2 * P], F16)
        centred = sb("centred", [P, 2 * P], F16)
        assert NTOK // 2 <= 2048
        oh_lo = xtok[:, :, :].rearrange("p b t -> p (b t)").bitcast(F16).rearrange("p (l n) -> p l n", l=LO)
        oh_hi = htok[:, :, :].rearrange("p b t -> p (b t)").bitcast(F16)[:, 0:HI * 2 * P]\
            .rearrange("p (h n) -> p h n", h=HI)
        idxf = sb("idxf", [LO, E * HI])
        idx = sb("idx", [P, E * NG], U32)

        gath = sb("gath", [P, E, NG, ROW])
        xt_flat = xtok[:, :, :].rearrange("p b t -> p (b t)")
        ht_flat = htok[:, :, :].rearrange("p b t -> p (b t)")
        n_x = 2 * KTOP
        xg = xt_flat[:, 0:n_x].rearrange("p (s n) -> p s n", s=2)
        yo = xt_flat[:, n_x:2 * n_x].rearrange("p (s k c) -> p s k c", s=2, k=NG)
        mid = ht_flat[:, 0:2 * len(FJ) * KTOP].rearrange("p (s j n) -> p s j n", s=2, j=len(FJ))

        tp = [pb("tp0", [P, T]), pb("tp1", [P, T])]
        mm = [pb("mm0", [P, T]), pb("mm1", [P, T])]
        mv_ps = pb("mv_ps", [P, T])
        moe = [pb("moe0", [P, T]), pb("moe1", [P, T])]
        small = pb("small", [P, T])
        lg = small[:, 0:NF * E].rearrange("p (f e) -> p f e", e=E)
        cps = small[:, NF * E:NF * E + 1]
        sel_ps = small[:, NF * E + 8:NF * E + 16]
        pt_ps = small[:, 0:W]
        sl_ps = tp[1]
        idx_ps = mv_ps[0:LO, 0:E * HI].rearrange("l (e h) -> l e h", e=E)
        kvr_ps = [(mm[0], mm[1], mv_ps), (moe[0], moe[1], tp[1])]
        kk_ps = [mm[0], mm[1], small]

        x_loaded = [sem(f"x_loaded{b}") for b in range(B)]
        w_loaded = sem("w_loaded")
        late_loaded = sem("late_loaded")
        base_copied = sem("base_copied")
        pool_step = sem("pool_step")
        consts_ready = sem("consts_ready")
        dve_step = sem("dve_step")
        act_step = sem("act_step")
        weights_ready = sem("weights_ready")
        mv_ready = sem("mv_ready")
        rs_ready = sem("rs_ready")
        xn_ready = sem("xn_ready")
        h_ready = sem("h_ready")
        rows_stored = sem("rows_stored")
        probs_stored = sem("probs_stored")
        xT_psum = sem("xT_psum")
        hT_psum = sem("hT_psum")
        xT_ready = sem("xT_ready")
        hT_ready = sem("hT_ready")
        lgT_psum = sem("lgT_psum")
        lgT_ready = sem("lgT_ready")
        logits_psum = sem("logits_psum")
        k_psum = sem("k_psum")
        v_psum = sem("v_psum")
        r_psum = sem("r_psum")
        k_ready = sem("k_ready")
        v_ready = sem("v_ready")
        r_ready = sem("r_ready")
        r_copied = sem("r_copied")
        m_ready = sem("m_ready")
        ab_ready = sem("ab_ready")
        relu_ready = sem("relu_ready")
        abexp_ready = sem("abexp_ready")
        s_ready = sem("s_ready")
        lns_ready = sem("lns_ready")
        e_ready = sem("e_ready")
        eexp_ready = sem("eexp_ready")
        aa_ready = sem("aa_ready")
        gates_ready = sem("gates_ready")
        x1_ready = sem("x1_ready")
        xp_ready = sem("xp_ready")
        lmax_ready = sem("lmax_ready")
        lexp_ready = sem("lexp_ready")
        prob_ready = sem("prob_ready")
        pcl_ready = sem("pcl_ready")
        pE_psum = sem("pE_psum")
        pE_ready = sem("pE_ready")
        cnt_ready = sem("cnt_ready")
        count_psum = sem("count_psum")
        ties_ready = sem("ties_ready")
        ties_psum = sem("ties_psum")
        selc_ready = sem("selc_ready")
        selc_psum = sem("selc_psum")
        slot_ready = sem("slot_ready")
        slot_psum = sem("slot_psum")
        onehot_ready = sem("onehot_ready")
        idx_psum = sem("idx_psum")
        idx_ready = sem("idx_ready")
        gathered = [sem(f"gathered{e}") for e in range(E)]
        up_psum = sem("up_psum")
        mid_ready = sem("mid_ready")
        mid_ones = sem("mid_ones")
        down_psum = sem("down_psum")
        yo_ready = sem("yo_ready")
        scattered = [sem("scattered0"), sem("scattered1")]
        yo_added = sem("yo_added")
        tp_filled = sem("tp_filled")
        tp_copied = sem("tp_copied")
        terms_ready = sem("terms_ready")
        xn2_ready = sem("xn2_ready")
        z_ready = sem("z_ready")
        rr_ready = sem("rr_ready")
        kk_psum = sem("kk_psum")
        kk_ready = sem("kk_ready")
        sq_ready = sem("sq_ready")
        dve_sq_ready = sem("dve_sq_ready")
        vv_psum = sem("vv_psum")
        x2_ready = sem("x2_ready")
        x2tok_psum = sem("x2tok_psum")
        x2tok_ready = sem("x2tok_ready")
        out_added = sem("out_added")

        loads = [(par[:, :], chan_cols), (wtm[:, :], W_tm),
                 (mixrow[:, :, :], chan_rows.rearrange("(o n) c -> o n c", o=1).broadcast_to([P, len(MIXES), C])),
                 (wr[:, :], Wr), (brc[:, :], br.rearrange("(e o) -> e o", o=1)),
                 (wcm[:, :], W_cm)]
        late = [(wcp[:, :, :], W_cp.rearrange("(j k) c -> k j c", j=NJ)),
                (wup[:, :, :], W_up.rearrange("g h f -> h g f"))]
        for j, fj in enumerate(FJ):
            late.append((bup[0:fj, :, j], b_up_t[P * j:P * j + fj, :]))
            late.append((wdn[0:fj, :, j, :], W_down[:, P * j:P * j + fj, :].rearrange("e f c -> f e c")))
        late.append((wdn[FJ[-1]:FJ[-1] + 1, :, len(FJ) - 1, :], b_down.rearrange("(o e) c -> o e c", o=1)))
        N_LOADS, N_LATE = 16 * len(loads), 16 * len(late)

        parts = [(0, 1), (2, 3, 4), (5, 6, 7)]
        rs_part = {b: n + 1 for n, mine in enumerate(parts) for b in mine}

        ORDER = [("ln", 0), ("ln", 1), ("gates", 0), ("ln", 2), ("fetch", 0), ("eexp", 0), ("eexp", 1),
                 ("ln", 3), ("widen", 0), ("gates", 1), ("fetch", 1), ("narrow", 0), ("widen", 1), ("fetch", 2),
                 ("fetch", 3), ("mix_terms", 0), ("narrow", 1), ("x1tok", 0), ("widen", 2), ("x1tok", 1),
                 ("gates", 2), ("fetch", 4), ("gates", 3), ("narrow", 2), ("widen", 3), ("xn2T", 0), ("eexp", 2),
                 ("fetch", 5), ("narrow", 3), ("eexp", 3), ("up", 0), ("widen", 4), ("squares", 0), ("xn2T", 1),
                 ("narrow", 4), ("down", 0), ("fetch", 6), ("widen", 5), ("x1tok", 2), ("mix_terms", 1),
                 ("narrow", 5), ("fetch", 7), ("widen", 6), ("up", 1), ("up", 2), ("rr", 0), ("mix_terms", 2),
                 ("squares", 1), ("narrow", 6), ("mix_terms", 3), ("x1tok", 3), ("down", 1), ("widen", 7),
                 ("up", 3), ("squares", 2), ("rr", 1), ("narrow", 7), ("xn2T", 2), ("down", 2), ("squares", 3),
                 ("x2tok", 0), ("up", 4), ("xn2T", 3), ("rr", 2), ("squares", 4), ("down", 3), ("x2tok", 1),
                 ("up", 5), ("squares", 5), ("rr", 3), ("down", 4), ("up", 6), ("down", 5), ("squares", 6),
                 ("up", 7), ("squares", 7), ("x2tok", 2), ("down", 6), ("x2tok", 3), ("x2tok", 4), ("x2tok", 5),
                 ("down", 7), ("x2tok", 6), ("x2tok", 7)]
        SPLIT_FROM = 7
        tp_turn = {}
        for kind, n in ORDER:
            for b in (2 * n, 2 * n + 1) if kind in ("x1tok", "xn2T") else (n,) if kind == "fetch" else ():
                tp_turn[kind, b] = len(tp_turn)

        act_squares = [(b, j) for b in range(B) for j in range(NJ) if b < SPLIT_FROM or j % 2 == 0]
        dve_squares = [(b, j) for b in range(B) for j in range(NJ) if (b, j) not in act_squares]

        def position(b):
            return (0 if b < 2 else len(EXP_STEPS) + 1 + TURN_STEPS * (b // 2 - 1)) + 3 * (b % 2)

        def rsqrt(engine, link, k, part):
            y, t, u = rs[:, 0:k, part], nt[:, 0:k, part], va[:, 0:k, part]
            link(engine.tensor_scalar(y.bitcast(I32), u.bitcast(I32), -0.5, float(0x5F3759DF), ALU.mult, ALU.add))
            for _ in range(3):
                link(engine.tensor_tensor(t, y, y, ALU.mult))
                if engine is nc.vector:
                    link(engine.scalar_tensor_tensor(t, t, -0.5, u, ALU.mult, ALU.mult))
                    link(engine.scalar_tensor_tensor(y, t, 1.5, y, ALU.add, ALU.mult))
                    continue
                link(engine.tensor_tensor(t, t, u, ALU.mult))
                link(engine.tensor_scalar(t, t, -0.5, 1.5, ALU.mult, ALU.add))
                link(engine.tensor_tensor(y, y, t, ALU.mult))

        block = ctx.enter_context(nc.Block())

        @block.sync
        def _(sp):
            def tiles(t, b):
                return t[:, b, :].rearrange("p (q c) -> p q c", q=Q)

            for b in range(B):
                sp.dma_start(tiles(xtok, b), x_v[b, :, :, :]).then_inc(x_loaded[b], 16)
            with nc.allow_non_contiguous_dma(reason="a few hundred bias values"):
                for dst, src in late:
                    sp.dma_start(dst, src).then_inc(late_loaded, 16)
            sp.dma_start(out.rearrange("b (h t) c -> (b h) (t c)", h=2),
                         x.rearrange("b (h t) c -> (b h) (t c)", h=2)).then_inc(base_copied, 16)
            with sp.Fori(0, PAIRS) as i:
                sp.wait_ge(xn_ready, i * 2 + 2)
                sp.dma_start(rows_v[:, bass.ts(i, 2 * Q), 0:C],
                             htok[:, bass.ts(i, 2), :].rearrange("p b (q c) -> p (b q) c", q=Q)).then_inc(rows_stored, 16)
            sp.wait_ge(prob_ready, 1)
            sp.dma_start(rows_v[:, :, C:ROW], prob[:, :, :]).then_inc(probs_stored, 16)
            sp.wait_ge(rows_stored, 16 * PAIRS)
            sp.wait_ge(probs_stored, 16)

        @block.gpsimd
        def _(pool):
            n = [0]

            def link(ins):
                n[0] += 1
                ins.then_inc(pool_step, 1)
                pool.wait_ge(pool_step, n[0])

            g = nc.gpsimd
            g.memset(st[:, :, 0:1], NEG_INF)
            g.memset(weps[:, :], WKV_EPS)
            g.memset(wrow[:, :], 1.0)
            g.memset(onesw[:, :], 1.0)
            g.memset(same[:, :], 1.0)
            link(g.memset(ident[:, :], 0.0))
            by_e = same[:, :].rearrange("k (e c) -> k e c", e=E)
            link(g.affine_select(out=by_e, in_=by_e, compare_op=ALU.is_ge, fill=0.0, base=0,
                                 pattern=[[-CH, E], [0, CH]], channel_multiplier=1))
            link(g.affine_select(out=by_e, in_=by_e, compare_op=ALU.is_ge, fill=0.0, base=CH - 1,
                                 pattern=[[CH, E], [0, CH]], channel_multiplier=-1))
            g.affine_select(out=earlier[:, :], in_=same[:, :], compare_op=ALU.is_gt, fill=0.0, base=0,
                            pattern=[[1, P]], channel_multiplier=-1)
            g.iota(centred[:, :].rearrange("p (l e c) -> p l e c", l=2, e=E), pattern=[[P, 2], [0, E], [2 * P, CH]],
                   base=-(NTOK // 2), channel_multiplier=1, allow_small_or_imprecise_dtypes=True)
            g.affine_select(out=ident[:, :], in_=ident[:, :], compare_op=ALU.not_equal, fill=1.0, base=0,
                            pattern=[[-1, P]], channel_multiplier=1).then_inc(consts_ready, 1)

            for k, mine in enumerate(parts):
                pool.wait_ge(mv_ready, k + 1)
                part = slice(mine[0] * Q, (mine[-1] + 1) * Q)
                g.tensor_scalar(va[:, 0, part], mv[:, part, 1], 1.0, LN_EPS, ALU.mult, ALU.add)
                link(g.tensor_scalar(va[:, 1, part], mv[:, part, 1], 1.0 + LN_EPS, LN_EPS * LN_EPS, ALU.mult, ALU.add))
                rsqrt(g, link, 2, part)
                link(g.tensor_tensor(nb[:, part], mv[:, part, 0], rs[:, 1, part], ALU.mult))
                g.tensor_scalar(nb[:, part], nb[:, part], -1.0, 0.0, ALU.mult, ALU.add).then_inc(rs_ready, 1)

            pool.wait_ge(w_loaded, N_LOADS)
            g.tensor_scalar(om[:, :], par[:, :], -1.0, 1.0, ALU.mult, ALU.add)
            g.tensor_scalar(negw[:, :], col["time_decay"], -1.0, 0.0, ALU.mult, ALU.add)
            g.tensor_scalar(wrow[:, :], wrow[:, :], col["time_decay"], None, ALU.mult)
            g.tensor_tensor(wtm[:, :], wtm[:, :], mixrow[:, 0:3, :].rearrange("p n c -> p (n c)"), ALU.mult)
            link(g.tensor_tensor(wcm[:, :].rearrange("p (j c) -> p j c", j=NJ), wcm[:, :].rearrange("p (j c) -> p j c", j=NJ),
                                 mixrow[:, 3:4, :].broadcast_to([P, NJ, C]), ALU.mult))
            pool.sem_inc(weights_ready, 1)

            pool.wait_ge(xp_ready, 1)
            pool.wait_ge(rows_stored, 16 * PAIRS)
            for b in range(B):
                link(g.tensor_scalar(htok[:, b, :], xT[:, b, 0:T], omc["tmr"], None, ALU.mult))
                pool.wait_ge(r_copied, b + 1)
                g.tensor_tensor(rb[:, b, :], rb[:, b, :], htok[:, b, :], ALU.add).then_inc(r_ready, 1)

            pool.wait_ge(probs_stored, 16)
            pool.wait_ge(base_copied, 16)
            pool.wait_ge(idx_ready, 1)

            def gather(e):
                for k in range(NG):
                    g.indirect_dma_start(out=gath[:, e, k, :], out_offset=None, in_=xn_rows[:, :],
                                         in_offset=bass.IndirectOffsetOnAxis(ap=idx[:, e * NG + k:e * NG + k + 1], axis=0),
                                         ).then_inc(gathered[e], 16)

            def scatter(e):
                s = e % 2
                pool.wait_ge(yo_ready, e + 1)
                for k in range(NG):
                    g.indirect_dma_start(out=out_rows,
                                         out_offset=bass.IndirectOffsetOnAxis(ap=idx[:, e * NG + k:e * NG + k + 1], axis=0),
                                         in_=yo[:, s, k, :], in_offset=None, compute_op=ALU.add).then_inc(scattered[s], 16)

            def landed(e):
                pool.wait_ge(scattered[e % 2], 16 * NG * (e // 2 + 1))
                pool.sem_inc(yo_added, 1)

            ahead = 4
            gather(0)
            gather(1)
            pool.wait_ge(idx_ready, 2)
            link(g.memset(mid[:, :, len(FJ) - 1, :], 1.0))
            pool.sem_inc(mid_ones, 1)
            for e in range(2, ahead):
                gather(e)
            for e in range(E):
                if e:
                    landed(e - 1)
                scatter(e)
                if e + ahead < E:
                    gather(e + ahead)
            landed(E - 1)
            for b in range(B):
                pool.wait_ge(x2tok_ready, b + 1)
                g.dma_start(out_v[b, :, :, :], ca[:, b, :].rearrange("p (q c) -> p q c", q=Q),
                            accum_op=ALU.add).then_inc(out_added, 16)
            pool.wait_ge(out_added, 16 * B)

        @block.scalar
        def _(act):
            a = nc.scalar
            for dst, src in loads:
                act.dma_start(dst, src).then_inc(w_loaded, 16)
            a.preload_act_table_set("natural_log_exp_and_others")
            for b in range(B + 1):
                if b < B:
                    act.wait_ge(xT_psum, b + 1)
                    a.copy(xT[:, b, 1:T + 1], tp[b % 2][:, :]).then_inc(xT_ready, 1)
                if b == 0:
                    act.wait_ge(w_loaded, N_LOADS)
                else:
                    act.wait_ge(lgT_psum, b)
                    a.activation(rb[0:E, b - 1, :], mm[(b - 1) % 2][0:E, :], ACT.Identity, bias=brc[:, 0:1]).then_inc(lgT_ready, 1)

            def h_token_major(b):
                act.wait_ge(rs_ready, rs_part[b])
                act.wait_ge(x_loaded[b], 16)
                for q in range(Q):
                    f = b * Q + q
                    last = a.activation(vb[:, b, P * q:P * q + P], xtok[:, b, P * q:P * q + P], ACT.Identity,
                                        bias=nb[:, f:f + 1], scale=rs[:, 1, f:f + 1])
                last.then_inc(h_ready, 1)

            h_token_major(0)
            act.wait_ge(lmax_ready, 1)
            a.activation(prob[:, :, :], prob[:, :, :], ACT.Exp).then_inc(lexp_ready, 1)
            def h_channel_major(b):
                act.wait_ge(hT_psum, b + 1)
                a.activation(ca[:, b, :], tp[b == 1][:, :], ACT.Identity, bias=col["b1"], scale=col["g1"]).then_inc(hT_ready, 1)

            def copy_r(b):
                act.wait_ge(r_psum, b + 1)
                a.copy(rb[:, b, :], kvr_ps[b % 2][2][:, :]).then_inc(r_copied, 1)

            def abexp(i):
                act.wait_ge(ab_ready, i + 1)
                act.wait_ge(r_psum, 2 * i + 2)
                a.activation(ca[:, 2 * i:2 * i + 2, :], kd[:, 2 * i:2 * i + 2, :], ACT.Relu, bias=negw[:, 0:1])
                a.activation(cb[:, 2 * i:2 * i + 2, :], kd[:, 2 * i:2 * i + 2, :], ACT.Relu, bias=col["time_decay"],
                             scale=-1.0).then_inc(relu_ready, 1)
                act.wait_ge(relu_ready, i + 1)
                a.activation(ca[:, 2 * i:2 * i + 2, :], ca[:, 2 * i:2 * i + 2, :], ACT.Exp, scale=-1.0)
                a.activation(cb[:, 2 * i:2 * i + 2, :], cb[:, 2 * i:2 * i + 2, :], ACT.Exp, scale=-1.0).then_inc(abexp_ready, 1)

            h_channel_major(0)
            h_token_major(1)
            h_channel_major(1)
            for i in range(PAIRS):
                for b in (2 * i, 2 * i + 1):
                    copy_r(b)
                    if b + 2 < B:
                        h_token_major(b + 2)
                        h_channel_major(b + 2)
                abexp(i)

            act.wait_ge(r_ready, B)
            for i in range(PAIRS):
                a.activation(rb[:, 2 * i:2 * i + 2, :], rb[:, 2 * i:2 * i + 2, :], ACT.Sigmoid)

            def ln(i):
                act.wait_ge(s_ready, 2 * i + 2)
                a.activation(st[:, 2 * i:2 * i + 2, 0:T], st[:, 2 * i:2 * i + 2, 0:T], ACT.Ln,
                             bias=weps[:, 0:1]).then_inc(lns_ready, 1)

            def eexp(i):
                act.wait_ge(e_ready, i + 1)
                a.activation(ca[:, 2 * i:2 * i + 2, :], ca[:, 2 * i:2 * i + 2, :], ACT.Exp, scale=-1.0)
                a.activation(cb[:, 2 * i:2 * i + 2, :], cb[:, 2 * i:2 * i + 2, :], ACT.Exp).then_inc(eexp_ready, 1)

            def gates(i):
                act.wait_ge(e_ready, i + 1)
                a.activation(kd[:, 2 * i:2 * i + 2, :], kd[:, 2 * i:2 * i + 2, :], ACT.Sigmoid, bias=col["time_first"])\
                    .then_inc(gates_ready, 1)

            def fetch(e):
                n = tp_turn["fetch", e]
                act.wait_ge(tp_filled, n + 1)
                if e == 0:
                    act.wait_ge(idx_psum, 2)
                a.copy(xg[:, e % 2, :], tp[n % 2][:, :]).then_inc(tp_copied, 1)

            def widen(e):
                if e == 0:
                    act.wait_ge(mid_ones, 1)
                    act.wait_ge(late_loaded, N_LATE)
                for j, fj in enumerate(FJ):
                    act.wait_ge(up_psum, e * len(FJ) + (j + 1))
                    a.activation(mid[0:fj, e % 2, j, :], moe[j % 2][0:fj, :], ACT.Silu,
                                 bias=bup[0:fj, e // EG, j:j + 1]).then_inc(mid_ready, 1)

            def narrow(e):
                act.wait_ge(down_psum, e + 1)
                if e >= 2:
                    act.wait_ge(yo_added, e - 1)
                for k in range(NG):
                    last = a.activation(yo[:, e % 2, k, :], moe[1][:, C * k:C * k + C], ACT.Copy,
                                        scale=gath[:, e, k, C + e:C + e + 1])
                last.then_inc(yo_ready, 1)

            def x1tok(i):
                for b in (2 * i, 2 * i + 1):
                    n = tp_turn["x1tok", b]
                    act.wait_ge(tp_filled, n + 1)
                    a.copy(ca[:, b, :], tp[n % 2][:, :]).then_inc(tp_copied, 1)

            def xn2T(i):
                for b in (2 * i, 2 * i + 1):
                    n = tp_turn["xn2T", b]
                    act.wait_ge(tp_filled, n + 1)
                    a.activation(rb[:, b, :], tp[n % 2][:, :], ACT.Identity, bias=col["b2"], scale=col["g2"])\
                        .then_inc(tp_copied, 1)

            def mix_terms(i):
                pr = slice(2 * i, 2 * i + 2)
                act.wait_ge(x1_ready, i + 1)
                a.activation(kd[:, pr, :], xT[:, pr, 0:T], ACT.Copy, scale=omc["cmk"])
                a.activation(cb[:, pr, :], xT[:, pr, 0:T], ACT.Copy, scale=omc["cmr"]).then_inc(terms_ready, 1)

            def rr(i):
                act.wait_ge(z_ready, i + 1)
                a.activation(cb[:, 2 * i:2 * i + 2, :], cb[:, 2 * i:2 * i + 2, :], ACT.Sigmoid).then_inc(rr_ready, 1)

            def squares(b):
                for j in range(NJ):
                    if (b, j) not in act_squares:
                        continue
                    n, z = act_squares.index((b, j)), rel[:, b % 2, j, :]
                    act.wait_ge(kk_ready, b * NJ + (j + 1))
                    a.activation(z, z, ACT.Relu).then_inc(act_step, 1)
                    act.wait_ge(act_step, n + 1)
                    a.activation(z, z, ACT.Square).then_inc(sq_ready, 1)

            def x2tok(b):
                act.wait_ge(x2tok_psum, b + 1)
                a.copy(ca[:, b, :], moe[b % 2][:, :]).then_inc(x2tok_ready, 1)

            table = "sigmoid"
            for kind, n in ORDER:
                if kind in ("ln", "eexp") and table != "ln and exp":
                    a.preload_act_table_set("natural_log_exp_and_others")
                table = {"ln": "ln and exp", "eexp": "ln and exp", "widen": "silu", "gates": "sigmoid",
                         "rr": "sigmoid"}.get(kind, table)
                {"ln": ln, "eexp": eexp, "gates": gates, "fetch": fetch, "widen": widen, "narrow": narrow,
                 "x1tok": x1tok, "xn2T": xn2T, "mix_terms": mix_terms, "rr": rr, "squares": squares, "x2tok": x2tok}.get(kind, lambda n: None)(n)

        @block.vector
        def _(dve):
            v = nc.vector
            steps = [0]
            per = [0, 0]

            def link(ins):
                per[0] += 1
                ins.then_inc(dve_step, 1)
                dve.wait_ge(dve_step, per[1] + (steps[0] + per[0]))

            def turn(i, size):
                steps[0] += per[0] if not isinstance(per[1], int) or per[1] == 0 else 0
                per[0], per[1] = 0, i * size

            def turned(size, turns):
                assert per[0] == size, (per[0], size)
                steps[0] += size * turns
                per[0], per[1] = 0, 0

            def statistics(t, b):
                for q in range(Q):
                    last = v.bn_stats(stats[:, b * Q + q, :], t[:, b, P * q:P * q + P])
                return last

            def aggregate(b):
                for q in range(Q):
                    last = v.bn_aggr(mv[:, b * Q + q, :], stats[:, b * Q + q, :])
                return last

            def normalise(dst, src, b, k):
                for q in range(Q):
                    f = b * Q + q
                    last = v.tensor_scalar(dst[:, b, P * q:P * q + P], src[:, b, P * q:P * q + P], mv[:, f, 0:1],
                                           rs[:, k, f:f + 1], ALU.subtract, ALU.mult)
                return last

            for n in range(len(parts) + 1):
                if n < len(parts):
                    for b in parts[n]:
                        dve.wait_ge(x_loaded[b], 16)
                        last = statistics(xtok, b)
                    link(last)
                    for b in parts[n]:
                        last = aggregate(b)
                    last.then_inc(mv_ready, 1)
                if n >= 1:
                    dve.wait_ge(rs_ready, n)
                    for b in parts[n - 1]:
                        normalise(htok, xtok, b, 0).then_inc(xn_ready, 1)

            def mix(dst, b, name, psum, psum_sem, ready, first=0):
                dve.wait_ge(psum_sem, b + (1 + first))
                v.scalar_tensor_tensor(dst[:, b, :], xT[:, b, 0:T], omc[name], psum[:, :],
                                       ALU.mult, ALU.add).then_inc(ready, 1)

            dve.wait_ge(logits_psum, B)
            link(v.tensor_reduce(rmax[:, :], lg, AX.X, ALU.max))
            v.tensor_tensor(prob[:, :, :], lg, rmax[:, :].unsqueeze(2).broadcast_to([P, NF, E]), ALU.subtract)\
                .then_inc(lmax_ready, 1)
            dve.wait_ge(xT_ready, B)
            v.tensor_copy(xT[:, :, 0:1], xT[:, :, 1:2]).then_inc(xp_ready, 1)
            dve.wait_ge(lexp_ready, 1)
            link(v.tensor_reduce(rmax[:, :], prob[:, :, :], AX.X, ALU.add))
            link(v.reciprocal(rmax[:, :], rmax[:, :]))
            v.tensor_tensor(prob[:, :, :], prob[:, :, :], rmax[:, :].unsqueeze(2).broadcast_to([P, NF, E]), ALU.mult)\
                .then_inc(prob_ready, 1)
            dve.wait_ge(prob_ready, 1)
            for h in range(2):
                last = v.tensor_scalar(pcl[:, h, :, :].rearrange("p e c -> p c e"), prob[:, h:NF:2, :], TINY, SCALE, ALU.max, ALU.mult)
            last.then_inc(pcl_ready, 1)

            def reach():
                with nc.allow_low_precision(reason="counts up to 256 are exact in bfloat16"):
                    v.tensor_scalar(hit[:, :], pE[:, :], cand[:, 0:1], 0.0, ALU.is_ge, ALU.add, accum_out=cnt[:, 0:1])\
                        .then_inc(cnt_ready, 1)

            def exponent_step(n):
                dve.wait_ge(count_psum, n + 1)
                h = EXP_STEPS[n] / 2
                if h >= 1:
                    link(v.tensor_scalar(ok[:, :], cps, KTOP - 0.5, 2.0 ** h - 2.0 ** -h, ALU.is_ge, ALU.mult))
                    link(v.scalar_tensor_tensor(cand[:, :], ok[:, :], 2.0 ** -h, cand[:, :], ALU.add, ALU.mult))
                    reach()

            def mantissa_step(n):
                dve.wait_ge(count_psum, n + len(EXP_STEPS) + 1)
                link(v.tensor_scalar(ok[:, :], cps, KTOP - 0.5, 0.5, ALU.is_ge, ALU.subtract))
                link(v.scalar_tensor_tensor(cand[:, :], ok[:, :], delta[:, 0:1], cand[:, :], ALU.mult, ALU.add))
                reach()
                v.tensor_scalar(delta[:, :], delta[:, :], 0.5, None, ALU.mult)

            def running_max(b):
                dve.wait_ge(k_ready, b + 1)
                v.tensor_tensor_scan(st[:, b, 1:T + 1], wrow[:, :], kd[:, b, :], NEG_INF,
                                     ALU.add, ALU.max).then_inc(m_ready, 1)

            def below_max(i):
                dve.wait_ge(m_ready, i * 2 + 2)
                v.tensor_tensor(kd[:, bass.ts(i, 2), :], kd[:, bass.ts(i, 2), :], st[:, bass.ts(i, 2), 0:T], ALU.subtract)\
                    .then_inc(ab_ready, 1)

            def mix_k(b, s):
                mix(kd, b, "tmk", kvr_ps[s][0], k_psum, k_ready)

            def mix_v(b, s):
                mix(vb, b, "tmv", kvr_ps[s][1], v_psum, v_ready)

            dve.wait_ge(xp_ready, 1)
            v.memset(cand[:, :], TINY * SCALE * 2.0 ** EXP_STEPS[0])
            dve.wait_ge(weights_ready, 1)
            dve.wait_ge(pE_psum, 1)
            link(v.tensor_copy(pE[:, :], pt_ps))
            dve.sem_inc(pE_ready, 1)
            reach()
            for b in range(2):
                mix_k(b, b)
                exponent_step(3 * b)
                mix_v(b, b)
                exponent_step(3 * b + 1)
                running_max(b)
                exponent_step(3 * b + 2)
            below_max(0)
            exponent_step(6)
            link(v.tensor_scalar(ok[:, :], cps, KTOP - 0.5, 0.5, ALU.is_ge, ALU.mult))
            link(v.scalar_tensor_tensor(cand[:, :], ok[:, :], 0.5, cand[:, :], ALU.add, ALU.mult))
            link(v.tensor_scalar(delta[:, :], cand[:, :], 0.5, None, ALU.mult))
            link(v.tensor_scalar(cand[:, :], cand[:, :], 1.5, None, ALU.mult))
            reach()
            mantissa_step(0)

            with dve.Fori(1, PAIRS) as i:
                turn(i - 1, 2 * TURN_STEPS)
                for s in range(2):
                    b = i * 2 + s
                    mix_k(b, s)
                    mantissa_step(i * TURN_STEPS + (3 * s + 1 - TURN_STEPS))
                    mix_v(b, s)
                    mantissa_step(i * TURN_STEPS + (3 * s + 2 - TURN_STEPS))
                    running_max(b)
                    mantissa_step(i * TURN_STEPS + (3 * s + 3 - TURN_STEPS))
                below_max(i)
                mantissa_step(i * TURN_STEPS)
            turned(2 * TURN_STEPS, PAIRS - 1)
            dve.wait_ge(count_psum, len(EXP_STEPS) + MAN_BITS)
            link(v.tensor_scalar(ok[:, :], cps, KTOP - 0.5, 1.0, ALU.is_ge, ALU.subtract))
            link(v.scalar_tensor_tensor(cand[:, :], ok[:, :], delta[:, 0:1], cand[:, :], ALU.mult, ALU.add))

            def exp_sum(b):
                dve.wait_ge(abexp_ready, b // 2 + 1)
                v.tensor_tensor_scan(st[:, b, 1:T + 1], ca[:, b, :], cb[:, b, :], 1.0, ALU.mult, ALU.add)\
                    .then_inc(s_ready, 1)

            with nc.allow_low_precision(reason="counts up to 256 are exact in bfloat16"):
                v.tensor_scalar(gt[:, :], pE[:, :], cand[:, 0:1], 0.0, ALU.is_gt, ALU.add, accum_out=gtc[:, 0:1])
                v.tensor_scalar(eq[:, :], pE[:, :], cand[:, 0:1], 0.0, ALU.is_equal, ALU.add, accum_out=eqc[:, 0:1])\
                    .then_inc(ties_ready, 1)
            link(v.memset(st[:, :, 0:1], 1.0))
            dve.wait_ge(ties_ready, 1)
            link(v.tensor_tensor_scan(rank[:, :], onesw[:, :], eq[:, :], 0.0, ALU.mult, ALU.add))
            dve.wait_ge(ties_psum, 1)
            link(v.tensor_scalar(need[:, :], sel_ps[:, 0:1], -1.0, float(KTOP), ALU.mult, ALU.add))
            link(v.tensor_tensor(need[:, :], need[:, :], sel_ps[:, 1:2], ALU.subtract))
            link(v.scalar_tensor_tensor(eq[:, :], rank[:, :], need[:, 0:1], eq[:, :], ALU.is_le, ALU.mult))
            link(v.tensor_tensor(gt[:, :], gt[:, :], eq[:, :], ALU.add))
            link(v.tensor_tensor_scan(rank[:, :], onesw[:, :], gt[:, :], 0.0, ALU.mult, ALU.add))
            v.tensor_copy(selc[:, :], rank[:, W - 1:W]).then_inc(selc_ready, 1)
            exp_sum(0)
            dve.wait_ge(selc_psum, 1)
            link(v.tensor_copy(need[:, :], sel_ps[:, 2:3]))
            v.scalar_tensor_tensor(eq[:, :], rank[:, :], need[:, 0:1], gt[:, :], ALU.add, ALU.mult).then_inc(slot_ready, 1)
            exp_sum(1)
            dve.wait_ge(slot_psum, 1)
            link(v.tensor_scalar(slot[:, :], sl_ps[:, 0:2 * P], -1.0, None, ALU.add))
            v.tensor_scalar(slot_hi[:, :], slot[:, :], 5, None, ALU.arith_shift_right)
            link(v.tensor_scalar(slot_lo[:, :], slot[:, :], LO - 1, None, ALU.bitwise_and))
            v.tensor_copy(hi16[:, :], slot_hi[:, :])
            link(v.tensor_copy(lo16[:, :], slot_lo[:, :]))
            dve.wait_ge(rows_stored, 16 * PAIRS)
            dve.wait_ge(h_ready, B)
            dve.wait_ge(r_ready, B)
            def experts_half(t, g):
                return t.rearrange("p (l n) -> p l n", l=2)[:, :, P // 2 * g:P // 2 * (g + 1)]

            def one_hot_hi(g):
                for h in range(HI):
                    last = v.tensor_scalar(experts_half(oh_hi[:, h, :], g), experts_half(hi16[:, :], g), float(h), None,
                                           ALU.is_equal)
                link(last)
                oh = oh_hi.rearrange("p h (l n) -> p h l n", l=2)
                for l in range(2):
                    half = slice(P // 2 * g, P // 2 * (g + 1))
                    v.tensor_tensor(oh[:, :, l, half], oh[:, :, l, half],
                                    centred[:, P * l:P * l + P][:, half].unsqueeze(1).broadcast_to([P, HI, P // 2]), ALU.mult)

            def one_hot_lo(g):
                for l in range(LO):
                    last = v.tensor_scalar(experts_half(oh_lo[:, l, :], g), experts_half(lo16[:, :], g), float(l), None,
                                           ALU.is_equal)
                last.then_inc(onehot_ready, 1)

            def indices(g):
                dve.wait_ge(idx_psum, g + 1)
                f_v = idxf[:, :].rearrange("l (e h) -> l e h", e=E)[:, E // 2 * g:E // 2 * (g + 1), :]
                link(v.tensor_scalar(f_v, idx_ps[:, E // 2 * g:E // 2 * (g + 1), :], float(NTOK // 2), None, ALU.add))
                f_g = idxf[:, :].rearrange("l (n j) -> l n j", j=P // LO)
                half = slice(E * NG // 2 * g, E * NG // 2 * (g + 1))
                for j in range(P // LO):
                    last = v.tensor_copy(idx[LO * j:LO * j + LO, half], f_g[:, half, j])
                last.then_inc(idx_ready, 1)

            one_hot_hi(0)
            one_hot_lo(0)
            one_hot_hi(1)
            exp_sum(2)
            indices(0)
            one_hot_lo(1)
            def above_state(i):
                pr = slice(2 * i, 2 * i + 2)
                dve.wait_ge(lns_ready, i + 1)
                link(v.tensor_tensor(kd[:, pr, :], kd[:, pr, :], st[:, pr, 0:T], ALU.subtract))
                v.tensor_scalar(ca[:, pr, :], kd[:, pr, :], col["time_decay"], 0.0, ALU.subtract, ALU.max)
                v.tensor_scalar(cb[:, pr, :], kd[:, pr, :], col["time_decay"], 0.0, ALU.subtract, ALU.min)\
                    .then_inc(e_ready, 1)

            def recurrence(i):
                pr = slice(2 * i, 2 * i + 2)
                v.memset(st[:, pr, 0:1], 0.0)
                dve.wait_ge(eexp_ready, i + 1)
                link(v.tensor_tensor(cb[:, pr, :], cb[:, pr, :], vb[:, pr, :], ALU.mult))
                for b in (2 * i, 2 * i + 1):
                    v.tensor_tensor_scan(st[:, b, 1:T + 1], ca[:, b, :], cb[:, b, :], 0.0, ALU.mult, ALU.add)\
                        .then_inc(aa_ready, 1)

            def attended(i):
                pr = slice(2 * i, 2 * i + 2)
                dve.wait_ge(gates_ready, i + 1)
                dve.wait_ge(aa_ready, i * 2 + 2)
                y, aa, x1 = ca[:, pr, :], st[:, pr, 0:T], xT[:, pr, 1:T + 1]
                link(v.tensor_tensor(y, vb[:, pr, :], aa, ALU.subtract))
                link(v.tensor_tensor(y, y, kd[:, pr, :], ALU.mult))
                link(v.tensor_tensor(y, y, aa, ALU.add))
                link(v.tensor_tensor(y, y, rb[:, pr, :], ALU.mult))
                link(v.tensor_tensor(x1, y, x1, ALU.add))
                v.tensor_copy(xT[:, pr, 0:1], xT[:, pr, T:T + 1]).then_inc(x1_ready, 1)

            def normalise_x1(i):
                mine = (2 * i, 2 * i + 1)
                for b in mine:
                    dve.wait_ge(tp_copied, tp_turn["x1tok", b] + 1)
                    last = statistics(ca, b)
                link(last)
                for b in mine:
                    last = aggregate(b)
                link(last)
                part = slice(mine[0] * Q, (mine[-1] + 1) * Q)
                link(v.tensor_scalar(va[:, 0, part], mv[:, part, 1], LN_EPS, None, ALU.add))
                rsqrt(v, link, 1, part)
                for b in mine:
                    normalise(ca, ca, b, 0).then_inc(xn2_ready, 1)

            def receptance(i):
                pr = slice(2 * i, 2 * i + 2)
                dve.wait_ge(tp_copied, tp_turn["xn2T", 2 * i + 1] + 1)
                dve.wait_ge(terms_ready, i + 1)
                v.scalar_tensor_tensor(cb[:, pr, :], rb[:, pr, :], col["cmr"], cb[:, pr, :], ALU.mult, ALU.add)\
                    .then_inc(z_ready, 1)

            def square(b, j):
                z = rel[:, b % 2, j, :]
                dve.wait_ge(kk_ready, NJ * b + j + 1)
                v.scalar_tensor_tensor(z, z, 0.0, z, ALU.max, ALU.mult).then_inc(dve_sq_ready, 1)

            def hidden(b):
                dve.wait_ge(terms_ready, b // 2 + 1)
                if b >= 2:
                    dve.wait_ge(vv_psum, b - 1)
                for j in range(NJ):
                    n = NJ * b + j
                    dve.wait_ge(kk_psum, n + 1)
                    v.tensor_tensor(rel[:, b % 2, j, :], kk_ps[n % 3][:, :], kd[:, b, :], ALU.add).then_inc(kk_ready, 1)
                    if (b, j - 1) in dve_squares:
                        square(b, j - 1)
                if (b, NJ - 1) in dve_squares:
                    square(b, NJ - 1)

            def x2(b):
                dve.wait_ge(vv_psum, b + 1)
                dve.wait_ge(rr_ready, b // 2 + 1)
                link(v.tensor_tensor(st[:, b, 0:T], mv_ps[:, :], cb[:, b, :], ALU.mult))
                v.tensor_tensor(st[:, b, 0:T], st[:, b, 0:T], xT[:, b, 1:T + 1], ALU.add).then_inc(x2_ready, 1)

            for stage, n in [(exp_sum, 3), (above_state, 0), (exp_sum, 4), (exp_sum, 5), (exp_sum, 6), (indices, 1),
                             (above_state, 1), (exp_sum, 7), (above_state, 2), (recurrence, 0), (attended, 0),
                             (recurrence, 1), (attended, 1), (above_state, 3), (normalise_x1, 0), (normalise_x1, 1),
                             (hidden, 0), (receptance, 0), (recurrence, 2), (attended, 2), (recurrence, 3),
                             (attended, 3), (receptance, 1), (hidden, 1), (hidden, 2), (x2, 0), (normalise_x1, 2),
                             (x2, 1), (hidden, 3), (normalise_x1, 3), (x2, 2), (hidden, 4), (receptance, 2), (x2, 3),
                             (hidden, 5), (receptance, 3), (x2, 4), (hidden, 6), (x2, 5), (hidden, 7), (x2, 6),
                             (x2, 7)]:
                stage(n)

        @block.tensor
        def _(pe):
            t = nc.tensor

            def wait(s, value):
                if value > 0:
                    pe.wait_ge(s, value)

            pe.wait_ge(consts_ready, 1)

            def logits(b):
                if b == 0:
                    pe.wait_ge(w_loaded, N_LOADS)
                wait(xT_ready, b + 1)
                wait(lgT_ready, b - 1)
                t.matmul(mm[b % 2][0:E, :], wr[:, :], xT[:, b, 1:T + 1], start=True, stop=True).then_inc(lgT_psum, 1)

            def logits_token_major(b):
                wait(lgT_ready, b + 1)
                for q in range(Q):
                    last = t.transpose(lg[:, Q * b + q, :], rb[0:E, b, P * q:P * q + P], ident[0:E, 0:E])
                last.then_inc(logits_psum, 1)

            for b in range(B + 2):
                if b < B:
                    wait(xn_ready, b + 1)
                    wait(xT_ready, b - 1)
                    for q in range(Q):
                        last = t.transpose(tp[b % 2][:, P * q:P * q + P], htok[:, b, P * q:P * q + P], ident[:, :])
                    last.then_inc(xT_psum, 1)
                if 1 <= b <= B:
                    logits(b - 1)
                if b >= 2:
                    logits_token_major(b - 2)

            def h_transposed(b):
                wait(h_ready, b + 1)
                wait(hT_ready, 1 if b == 2 else b if b > 2 else 0)
                for q in range(Q):
                    last = t.transpose(tp[b == 1][:, P * q:P * q + P], vb[:, b, P * q:P * q + P], ident[:, :])
                last.then_inc(hT_psum, 1)

            def kvr(b, n):
                ready, done = ((k_ready, k_psum), (v_ready, v_psum), (r_copied, r_psum))[n]
                wait(hT_ready, b + 1)
                wait(ready, b - 1)
                t.matmul(kvr_ps[b % 2][n][:, :], wtm[:, C * n:C * n + C], ca[:, b, :], start=True, stop=True).then_inc(done, 1)

            h_transposed(0)
            pe.wait_ge(weights_ready, 1)
            kvr(0, 0)
            pe.wait_ge(pcl_ready, 1)
            for h in range(2):
                last = t.transpose(pt_ps[:, P * h:P * h + P], pcl[:, h, :, :].rearrange("p e c -> p (e c)"), ident[:, :])
            last.then_inc(pE_psum, 1)
            pe.wait_ge(pE_ready, 1)
            start = {0: -1} | {b: max(position(b) - 3, 2) for b in range(1, B)}
            for n in range(len(EXP_STEPS) + MAN_BITS):
                pe.wait_ge(cnt_ready, n + 1)
                t.matmul(cps, same[:, :], cnt[:, :], start=True, stop=True).then_inc(count_psum, 1)
                for b in range(B):
                    if b and n == start[b] - 2:
                        h_transposed(b)
                    if 0 <= n - start[b] < 3:
                        kvr(b, n - start[b])

            pe.wait_ge(ties_ready, 1)
            t.matmul(sel_ps[:, 0:1], same[:, :], gtc[:, :], start=True, stop=True)
            t.matmul(sel_ps[:, 1:2], earlier[:, :], eqc[:, :], start=True, stop=True).then_inc(ties_psum, 1)
            pe.wait_ge(selc_ready, 1)
            t.matmul(sel_ps[:, 2:3], earlier[:, :], selc[:, :], start=True, stop=True).then_inc(selc_psum, 1)
            pe.wait_ge(slot_ready, 1)
            pe.wait_ge(r_copied, B)
            for h in range(2):
                last = t.transpose(sl_ps[:, P * h:P * h + P], eq[:, P * h:P * h + P], ident[:, :])
            last.then_inc(slot_psum, 1)

            for e in range(E):
                if e % (E // 2) == 0:
                    pe.wait_ge(onehot_ready, e // (E // 2) + 1)
                for f in range(NF):
                    n = (f % 2) * P + e * CH + f // 2
                    last = t.matmul(idx_ps[:, e, :], oh_lo[:, :, n], oh_hi[:, :, n],
                                    start=(f == 0), stop=(f == NF - 1))
                if e % (E // 2) == E // 2 - 1:
                    last.then_inc(idx_psum, 1)

            def transposed(kind, b, src):
                n = tp_turn[kind, b]
                wait(tp_copied, n - 1)
                for q in range(Q):
                    last = t.transpose(tp[n % 2][:, P * q:P * q + P], src[:, P * q:P * q + P], ident[:, :])
                last.then_inc(tp_filled, 1)

            def fetch(e):
                pe.wait_ge(gathered[e], 16 * NG)
                n = tp_turn["fetch", e]
                wait(tp_copied, n - 1)
                for k in range(NG):
                    last = t.transpose(tp[n % 2][:, P * k:P * k + P], gath[:, e, k, 0:C], ident[:, :])
                last.then_inc(tp_filled, 1)

            def widen(e):
                if e == 0:
                    pe.wait_ge(late_loaded, N_LATE)
                wait(tp_copied, tp_turn["fetch", e] + 1)
                for j, fj in enumerate(FJ):
                    if j == 0:
                        wait(mid_ready, len(FJ) * e)
                    if j == 1:
                        wait(yo_ready, e)
                    if j == 2:
                        wait(mid_ready, len(FJ) * e + 1)
                    t.matmul(moe[j % 2][0:fj, :], wup[:, e // EG, P * j:P * j + fj], xg[:, e % 2, :],
                             start=True, stop=True).then_inc(up_psum, 1)

            def narrow(e):
                wait(mid_ready, len(FJ) * (e + 1))
                for k in range(NG):
                    for j, fj in enumerate(FJ):
                        rows = fj + (j == len(FJ) - 1)
                        last = t.matmul(moe[1][:, C * k:C * k + C], mid[0:rows, e % 2, j, P * k:P * k + P],
                                        wdn[0:rows, e, j, :], start=(j == 0), stop=(j == len(FJ) - 1))
                last.then_inc(down_psum, 1)

            def x1tok(i):
                pe.wait_ge(x1_ready, i + 1)
                for b in (2 * i, 2 * i + 1):
                    transposed("x1tok", b, xT[:, b, 1:T + 1])

            def xn2T(i):
                for b in (2 * i, 2 * i + 1):
                    pe.wait_ge(xn2_ready, b + 1)
                    transposed("xn2T", b, ca[:, b, :])

            def up(b):
                wait(tp_copied, tp_turn["xn2T", b] + 1)
                for j in range(NJ):
                    n = NJ * b + j
                    wait(kk_ready, n - 2)
                    t.matmul(kk_ps[n % 3][:, :], wcm[:, C * j:C * j + C], rb[:, b, :], start=True, stop=True).then_inc(kk_psum, 1)

            def down(b):
                wait(x2_ready, b)
                for j in range(NJ):
                    if (b, j) in act_squares:
                        wait(sq_ready, act_squares.index((b, j)) + 1)
                    else:
                        wait(dve_sq_ready, dve_squares.index((b, j)) + 1)
                    last = t.matmul(mv_ps[:, :], wcp[:, j, :], rel[:, b % 2, j, :], start=(j == 0), stop=(j == NJ - 1))
                last.then_inc(vv_psum, 1)

            def x2tok(b):
                pe.wait_ge(x2_ready, b + 1)
                wait(yo_ready, E)
                wait(x2tok_ready, b - 1)
                for q in range(Q):
                    last = t.transpose(moe[b % 2][:, P * q:P * q + P], st[:, b, P * q:P * q + P], ident[:, :])
                last.then_inc(x2tok_psum, 1)

            for kind, n in ORDER:
                {"fetch": fetch, "widen": widen, "narrow": narrow, "x1tok": x1tok, "xn2T": xn2T, "up": up, "down": down, "x2tok": x2tok}\
                    .get(kind, lambda n: None)(n)


def kernel(**inputs):
    import numpy as _np
    import concourse.bacc as _bacc
    from concourse import mybir as _mybir
    from concourse.bass_utils import run_bass_kernel_spmd as _run

    nc = _bacc.Bacc("TRN2", target_bir_lowering=False, num_devices=1)
    given = {n[len("L0_"):]: _np.asarray(a) for n, a in inputs.items()}
    chan = {n: given["attn_" + n].reshape(-1) for n in PARAMS}
    laid_out = {
        "x": given["attn_x"],
        "chan_cols": _np.stack([chan[n] for n in PARAMS], axis=1),
        "chan_rows": _np.stack([chan[n] for n in MIXES]),
        "W_tm": given["attn_W_tm"], "W_cm": given["attn_W_cm"], "W_cp": given["attn_W_cp"],
        "Wr": given["ffn_Wr"], "br": given["ffn_br"], "W_up": given["ffn_W_up"], "b_up_t": given["ffn_b_up"].T,
        "W_down": given["ffn_W_down"], "b_down": given["ffn_b_down"],
    }
    arrays, args = {}, []
    for name, a in laid_out.items():
        a = _np.ascontiguousarray(a)
        arrays[f"in_{name}"] = a
        args.append(nc.dram_tensor(f"in_{name}", a.shape, _mybir.dt.from_np(a.dtype), kind="ExternalInput").ap())
    shape = laid_out["x"].shape
    args.append(nc.dram_tensor("out_0", shape, _mybir.dt.float32, kind="ExternalOutput").ap())
    rwkv_plus_expert_choice(nc, *args)
    r = _run(nc, [arrays], core_ids=[0])
    return r.results[0]["out_0"]
```
